# Optimizing a Trainium2 kernel written in Bass

```python
import numpy as np
import jax
import jax.numpy as jnp

def _softmax(x, axis=-1):
    return jax.nn.softmax(x, axis=axis)

def _gelu(x):
    return jax.nn.gelu(x, approximate=True)

def _silu(x):
    return jax.nn.silu(x)

def _sigmoid(x):
    return jax.nn.sigmoid(x)

def _layernorm(x, axis=-1, eps=1e-05):
    m = jnp.mean(x, axis=axis, keepdims=True)
    v = jnp.var(x, axis=axis, keepdims=True)
    return (x - m) / jnp.sqrt(v + eps)

def _scatter_add(tgt, idx, src, axis=0):
    return tgt.at[idx].add(src)

def _segment_sum(src, seg, n):
    return jax.ops.segment_sum(src, seg, n)
kernel_name = 'mk_flamingo_gated_d1_seqx_r4_cb7323'

def setup_inputs(seed: int=0):
    np.random.seed(seed)
    _w = jnp.asarray

    def _rec_inputs():
        import jax
        import jax.numpy as jnp
        _rk = jax.random.key(seed)
        x = -0.0002928 + 1 * jax.random.normal(jax.random.fold_in(_rk, 1), (16, 128, 256), jnp.float32)
        _lenS = 128 - jax.random.randint(jax.random.fold_in(_rk, 7), (16,), 0, max(1, 128 // 4) + 1, jnp.int32)
        _lenS2 = 128 - jax.random.randint(jax.random.fold_in(_rk, 8), (16,), 0, max(1, 128 // 4) + 1, jnp.int32)
        _ctx_768P = jax.random.normal(jax.random.fold_in(_rk, 11), (16, 16, 192), jnp.float32)
        _ctx_768c = jax.random.dirichlet(jax.random.fold_in(_rk, 511), 0.3 * jnp.ones((16,), jnp.float32), (16, 128))
        _ctx_768t = jnp.einsum('bsk,bkd->bsd', _ctx_768c, _ctx_768P)
        _ctx_768t = _ctx_768t * jax.lax.rsqrt(jnp.mean(jnp.square(_ctx_768t)) + 1e-12) * 0.953939
        ctx_768 = 2.09791e-05 + 1.00001 * (_ctx_768t + 0.3 * jax.random.normal(jax.random.fold_in(_rk, 611), (16, 128, 192), jnp.float32))
        _validS = jnp.arange(128)[None, :] < _lenS[:, None]
        _validS2 = jnp.arange(128)[None, :] < _lenS2[:, None]
        _causal = jnp.tril(jnp.ones((128, 128), dtype=bool))
        mask_BxS2_bf1 = jnp.ones((16, 128), dtype=bool)
        _g = jax.random.normal(jax.random.fold_in(_rk, 9001), (2, 1), jnp.float32)
        _g = jnp.sign(_g) * jnp.maximum(jnp.abs(_g), 1.0) + (_g == 0) * 1.0
        g_xattn = _g[0]
        g_ffn = _g[1]
        return (x, ctx_768, mask_BxS2_bf1, g_xattn, g_ffn)
    x, ctx_768, mask_BxS2_bf1, g_xattn, g_ffn = _rec_inputs()

    def _L0_xattn_setup():
        import jax, jax.numpy as jnp
        import numpy as np
        import math
        B, N, M = (4, 256, 256)
        DIM, CTX_DIM = (256, 192)
        HEADS, DIM_HEAD = (16, 64)
        INNER = HEADS * DIM_HEAD

        def layer_norm(t, g, eps=1e-05):
            mean = jnp.mean(t, axis=-1, keepdims=True)
            var = jnp.mean((t - mean) ** 2, axis=-1, keepdims=True)
            return (t - mean) * jax.lax.rsqrt(var + eps) * g
        key = jax.random.key(seed)
        ks = jax.random.split(key, 8)
        return {'x': jax.random.normal(ks[0], (B, N, DIM), jnp.float32), 'context': jax.random.normal(ks[1], (B, M, CTX_DIM), jnp.float32), 'mask': jnp.ones((B, M), dtype=bool), 'g_norm': jnp.ones((DIM,), jnp.float32), 'null_kv': jax.random.normal(ks[2], (2, DIM_HEAD), jnp.float32), 'Wq': jax.random.normal(ks[3], (DIM, INNER), jnp.float32) * DIM ** (-0.5), 'Wkv': jax.random.normal(ks[4], (CTX_DIM, 2 * INNER), jnp.float32) * CTX_DIM ** (-0.5), 'Wout': jax.random.normal(ks[5], (INNER, DIM), jnp.float32) * INNER ** (-0.5), 'g_out': jnp.ones((DIM,), jnp.float32)}
    _L0_xattn_all = _L0_xattn_setup()
    _L0_xattn_in = {k: v for k, v in _L0_xattn_all.items() if k in ('g_norm', 'null_kv', 'Wq', 'Wkv', 'Wout', 'g_out')}
    del _L0_xattn_all

    def _L0_ffn_setup():
        import jax, jax.numpy as jnp
        import numpy as np
        B, S, D, E, F = (2, 512, 256, 8, 1024)
        key = jax.random.key(seed)
        ks = jax.random.split(key, 4)
        return {'hidden_states': jax.random.normal(ks[0], (B, S, D), dtype=jnp.float32), 'Wr': jax.random.normal(ks[1], (D, E), dtype=jnp.float32) * (1.0 / np.sqrt(D)), 'W1': jax.random.normal(ks[2], (E, D, F), dtype=jnp.float32) * (1.0 / np.sqrt(D)), 'b1': jnp.zeros((E, F), dtype=jnp.float32), 'W2': jax.random.normal(ks[3], (E, F, D), dtype=jnp.float32) * (1.0 / np.sqrt(F)), 'b2': jnp.zeros((E, D), dtype=jnp.float32)}
    _L0_ffn_all = _L0_ffn_setup()
    _L0_ffn_in = {k: v for k, v in _L0_ffn_all.items() if k in ('Wr', 'W1', 'b1', 'W2', 'b2')}
    del _L0_ffn_all
    return {'x': x, 'ctx_768': ctx_768, 'mask_BxS2_bf1': mask_BxS2_bf1, 'g_xattn': g_xattn, 'g_ffn': g_ffn, 'L0_xattn_g_norm': _L0_xattn_in['g_norm'], 'L0_xattn_null_kv': _L0_xattn_in['null_kv'], 'L0_xattn_Wq': _L0_xattn_in['Wq'], 'L0_xattn_Wkv': _L0_xattn_in['Wkv'], 'L0_xattn_Wout': _L0_xattn_in['Wout'], 'L0_xattn_g_out': _L0_xattn_in['g_out'], 'L0_ffn_Wr': _L0_ffn_in['Wr'], 'L0_ffn_W1': _L0_ffn_in['W1'], 'L0_ffn_b1': _L0_ffn_in['b1'], 'L0_ffn_W2': _L0_ffn_in['W2'], 'L0_ffn_b2': _L0_ffn_in['b2']}

def reference(x, ctx_768, mask_BxS2_bf1, g_xattn, g_ffn, L0_xattn_g_norm, L0_xattn_null_kv, L0_xattn_Wq, L0_xattn_Wkv, L0_xattn_Wout, L0_xattn_g_out, L0_ffn_Wr, L0_ffn_W1, L0_ffn_b1, L0_ffn_W2, L0_ffn_b2):
    import jax
    import jax.numpy as jnp

    def _L0_xattn_ref(x, context, mask, g_norm, null_kv, Wq, Wkv, Wout, g_out):
        import jax, jax.numpy as jnp
        import numpy as np
        import math
        B, N, M = (4, 256, 256)
        DIM, CTX_DIM = (256, 192)
        HEADS, DIM_HEAD = (16, 64)
        INNER = HEADS * DIM_HEAD

        def layer_norm(t, g, eps=1e-05):
            mean = jnp.mean(t, axis=-1, keepdims=True)
            var = jnp.mean((t - mean) ** 2, axis=-1, keepdims=True)
            return (t - mean) * jax.lax.rsqrt(var + eps) * g
        b = x.shape[0]
        scale = DIM_HEAD ** (-0.5)
        sqrt_scale = math.sqrt(scale)
        x = layer_norm(x, g_norm)
        q = x @ Wq
        kv = context @ Wkv
        k, v = jnp.split(kv, 2, axis=-1)

        def to_heads(t):
            return t.reshape(b, t.shape[1], HEADS, DIM_HEAD).transpose(0, 2, 1, 3)
        q, k, v = (to_heads(q), to_heads(k), to_heads(v))
        nk = jnp.broadcast_to(null_kv[0], (b, HEADS, 1, DIM_HEAD))
        nv = jnp.broadcast_to(null_kv[1], (b, HEADS, 1, DIM_HEAD))
        k = jnp.concatenate([nk, k], axis=2)
        v = jnp.concatenate([nv, v], axis=2)
        q = q * sqrt_scale
        k = k * sqrt_scale
        sim = jnp.einsum('bhid,bhjd->bhij', q, k)
        max_neg = -jnp.finfo(sim.dtype).max
        full_mask = jnp.pad(mask, ((0, 0), (1, 0)), constant_values=True)
        sim = jnp.where(full_mask[:, None, None, :], sim, max_neg)
        attn = jax.nn.softmax(sim.astype(jnp.float32), axis=-1).astype(sim.dtype)
        out = jnp.einsum('bhij,bhjd->bhid', attn, v)
        out = out.transpose(0, 2, 1, 3).reshape(b, -1, INNER)
        out = out @ Wout
        return layer_norm(out, g_out)

    def _L0_ffn_ref(hidden_states, Wr, W1, b1, W2, b2):
        import jax, jax.numpy as jnp
        import numpy as np
        B, S, D, E, F = (2, 512, 256, 8, 1024)
        b, s, d = hidden_states.shape
        e = Wr.shape[1]
        x = hidden_states.reshape(b * s, d)
        router_logits = x @ Wr
        router_probs = jax.nn.softmax(router_logits, axis=-1)
        expert_idx = jnp.argmax(router_probs, axis=-1)
        p_max = jnp.max(router_probs, axis=-1, keepdims=True)

        def expert_mlp(w1, bb1, w2, bb2):
            h = jax.nn.gelu(x @ w1 + bb1, approximate=False)
            return h @ w2 + bb2
        outs = jax.vmap(expert_mlp)(W1, b1, W2, b2)
        onehot = jax.nn.one_hot(expert_idx, e, dtype=x.dtype)
        next_states = jnp.einsum('te,etd->td', onehot, outs)
        out = p_max * next_states
        return out.reshape(b, s, d)
    x = x + jnp.tanh(g_xattn[0]) * _L0_xattn_ref(_layernorm(x, axis=-1), ctx_768, mask_BxS2_bf1, L0_xattn_g_norm, L0_xattn_null_kv, L0_xattn_Wq, L0_xattn_Wkv, L0_xattn_Wout, L0_xattn_g_out)
    x = x + jnp.tanh(g_ffn[0]) * _L0_ffn_ref(_layernorm(x, axis=-1), L0_ffn_Wr, L0_ffn_W1, L0_ffn_b1, L0_ffn_W2, L0_ffn_b2)
    return x

_drawn_inputs = setup_inputs


def setup_inputs(seed=0):
    import zlib

    import numpy as np

    out = dict(_drawn_inputs(seed))
    spreads = {'L0_xattn_g_norm': (1.0, 0.2),
     'L0_xattn_g_out': (1.0, 0.2),
     'L0_ffn_b1': (0.0, 0.418),
     'L0_ffn_b2': (0.0, 0.285)}
    factors = {}
    for name, (base, spread) in spreads.items():
        noise = np.random.default_rng([zlib.crc32(name.encode()), seed]).standard_normal(out[name].shape)
        drawn = base * np.exp(spread * noise) if base else spread * noise
        out[name] = jnp.asarray(drawn.astype(out[name].dtype))
    for name, factor in factors.items():
        out[name] = (out[name] * factor).astype(out[name].dtype)
    return out
```

```python
from contextlib import ExitStack

import concourse.bass as bass
from concourse import mybir

P = 128
ALU = mybir.AluOpType
ACT = mybir.ActivationFunctionType
F32 = mybir.dt.float32
BF16 = mybir.dt.bfloat16
I32 = mybir.dt.int32
U8 = mybir.dt.uint8
AX_X = mybir.AxisListType.X
EPS = 1e-5
CREDIT = 1
MASKED = 1e30
ds = bass.ds


def flamingo_layer(nc, x, ctx_in, mask, g_xattn, g_ffn, g_norm, null_kv, w_q, w_kv, w_out,
                   g_out, w_r, w_1, b_1, w_2, b_2, out):
    B, N, D = x.shape
    C = ctx_in.shape[2]
    INNER = w_q.shape[1]
    DH = null_kv.shape[1]
    H = INNER // DH
    E, F = b_1.shape
    assert N == P and ctx_in.shape[1] == P and 2 * DH == P
    KD = D // P
    CC = C // 2
    HP = H // 2
    GT = 4
    NG = B // GT
    SCALE = DH ** -0.5
    FC = F // P
    NS = B + E - 1
    NSP = -(-NS // 4) * 4
    NB = 4

    with ExitStack() as ctx:
        def sb(name, shape, dt=F32):
            return ctx.enter_context(nc.sbuf_tensor(name, shape, dt))

        def sem(name):
            return ctx.enter_context(nc.semaphore(name))

        h2_sorted = nc.dram_tensor("h2_sorted", (NSP * P, D), F32).ap()
        y_sorted = nc.dram_tensor("y_sorted", (NS * P, D), F32).ap()

        x_sb = sb("x_sb", [P, B, D])
        xn_sb = sb("xn_sb", [P, B, D])
        att_sb = sb("att_sb", [P, B, D])
        xT = sb("xT", [P, KD, B * P])
        arena = sb("arena", [P, 26624])
        used = [0]

        def carve(cols):
            used[0] += cols
            assert used[0] <= 26624
            return arena[:, used[0] - cols:used[0]]

        ctx_sb = carve(B * C).rearrange("p (b c) -> p b c", b=B)
        ctxT = carve(2 * B * P).rearrange("p (c t) -> p c t", c=2)
        ctx_cur = carve(2 * GT * P).rearrange("p (c t) -> p c t", c=2)
        wq_sb = carve(KD * INNER).rearrange("p (k n) -> p k n", k=KD)
        wkv_sb = carve(4 * INNER).rearrange("p (c n) -> p c n", c=2)
        wout_sb = carve(HP * D).rearrange("p (c n) -> p c n", c=HP)
        qT = carve(GT * P)
        kT = carve(GT * 2 * P).rearrange("p (b n) -> p b n", b=GT)
        v_sb = [carve(GT * P).rearrange("p (b n) -> p b n", b=GT) for _ in range(2)]
        probs = carve(GT * 2 * P).rearrange("p (j n) -> p j n", j=2 * GT)
        probsT = carve(GT * 2 * P).rearrange("p (j n) -> p j n", j=2 * GT)
        oT = carve(GT * P)
        used[0] = 0
        w1_sb = [carve(KD * F).rearrange("p (k n) -> p k n", k=KD) for _ in range(NB)]
        w2_sb = [carve(FC * D).rearrange("p (c n) -> p c n", c=FC) for _ in range(NB)]
        b2_sb = [carve(D) for _ in range(NB)]
        hT = [carve(FC * P).rearrange("p (c n) -> p c n", c=FC) for _ in range(2)]
        xs_sb = [carve(D) for _ in range(NB)]
        xsT = [carve(KD * P).rearrange("p (k n) -> p k n", k=KD) for _ in range(2)]
        y_sb = [carve(D) for _ in range(2)]
        b1_cur = [carve(FC) for _ in range(2)]

        ident = sb("ident", [P, P])
        zeros = sb("zeros", [P, 1024])
        row0_one = sb("row0_one", [P, P], BF16)
        mask_u8 = sb("mask_u8", [1, B * P], U8)
        mask_bias = sb("mask_bias", [P, B, P], BF16)
        before = sb("before", [P, P], BF16)
        ones_bf = sb("ones_bf", [P, P], BF16)
        gout_row = sb("gout_row", [P, D])
        nk_row = sb("nk_row", [P, DH])
        wr_sb = sb("wr_sb", [P, KD, E])
        gates = sb("gates", [P, 2])
        tanhs = sb("tanhs", [P, 2])
        stats = sb("stats", [P, B, 6])
        mv = sb("mv", [P, B, 2])
        rstd = sb("rstd", [P, B])
        minus_half = sb("minus_half", [P, B])
        wqn = sb("wqn", [P, KD, H])
        wq_nk = att_sb[:, 0:KD * INNER // D, :]
        nv_diag = sb("nv_diag", [P, HP, P])
        rows_of = sb("rows_of", [P, GT])
        nw_rows = sb("nw_rows", [P, GT, D])
        nsn = sb("nsn", [P, B, H])
        nmax = sb("nmax", [P, GT, 2])
        rowmax = sb("rowmax", [P, GT, 2])
        null_diff = sb("null_diff", [P, GT, 2])
        null_exp = sb("null_exp", [P, GT, 2])
        sums = sb("sums", [P, GT, 2])
        denom = sb("denom", [P, GT, 2])
        recip = sb("recip", [P, GT, 2])
        null_p = sb("null_p", [P, P])
        null_pT = sb("null_pT", [P, P])
        logits = sb("logits", [P, B, E])
        onehot = sb("onehot", [P, B, E], BF16)
        r_a = sb("r_a", [P, B, E])
        r_b = sb("r_b", [P, B, E])
        r_max = sb("r_max", [P, B])
        r_sum = sb("r_sum", [P, B])
        coef = sb("coef", [P, B])
        first = sb("first", [P, B])
        iota_i = sb("iota_i", [P, NS], I32)
        iota_s = sb("iota_s", [P, NS])
        iota_e8 = sb("iota_e8", [P, E])
        keep_scan = sb("keep_scan", [P, E, B])
        counts = sb("counts", [P, E, B])
        upto = sb("upto", [P, E, B])
        tiles_i = sb("tiles_i", [P, E], I32)
        tiles_n = sb("tiles_n", [P, E])
        ones_e = sb("ones_e", [P, E])
        ends = sb("ends", [P, E])
        starts = sb("starts", [P, E])
        base = sb("base", [P, E, B])
        pos_f = sb("pos_f", [P, B])
        pos_i = sb("pos_i", [P, B], I32)
        past = sb("past", [P, NS, E])
        eid_f = sb("eid_f", [P, NS])
        eid_i = sb("eid_i", [P, NS], I32)
        as_rows = sb("as_rows", [P, P])
        as_cols = sb("as_cols", [P, P])
        b1T = as_cols[:, 0:E * FC]
        gn_col = as_cols[:, E * FC:E * FC + KD]
        nv_col = as_cols[:, E * FC + KD:E * FC + KD + 1]

        bank = [ctx.enter_context(nc.psum_tensor(f"bank{i}", [P, 512], F32)) for i in range(3)]
        ps_s = ctx.enter_context(nc.psum_tensor("ps_s", [P, 1024], F32))
        ps_acc = ctx.enter_context(nc.psum_tensor("ps_acc", [P, 1024], F32))
        ps_o = ctx.enter_context(nc.psum_tensor("ps_o", [P, 512], F32))
        ps_q, ps_k, ps_v = bank
        banks = [ps_q[:, :], ps_k[:, :], ps_v[:, :], ps_s[:, 0:512], ps_s[:, 512:1024],
                 ps_o[:, :], ps_acc[:, 0:512], ps_acc[:, 512:1024]]

        x_in = [sem(f"x_in{g}") for g in range(NG)]
        c_in = [sem(f"c_in{g}") for g in range(NG)]
        small_in = sem("small_in")
        wq_in = sem("wq_in")
        wkv_in = sem("wkv_in")
        wout_in = sem("wout_in")
        zeroed = sem("zeroed")
        scattered = sem("scattered")
        w1_in = [sem(f"w1_in{j}") for j in range(NB)]
        w2_in = [sem(f"w2_in{j}") for j in range(NB)]
        b2_in = [sem(f"b2_in{j}") for j in range(NB)]
        xs_in = [sem(f"xs_in{j}") for j in range(NB)]
        y_stored = [sem(f"y_stored{j}") for j in range(2)]
        gathered = [sem(f"gathered{t}") for t in range(4)]
        out_stored = sem("out_stored")
        pool_made = sem("pool_made")
        rows_clear = sem("rows_clear")
        cols_ps = sem("cols_ps")
        cols_ready = sem("cols_ready")
        pow_done = sem("pow_done")
        var_ready = sem("var_ready")
        dve_chain = sem("dve_chain")
        xn_ready = sem("xn_ready")
        turned = sem("turned")
        copied_act = sem("copied_act")
        copied_dve = sem("copied_dve")
        act_setup = sem("act_setup")
        mask_ready = sem("mask_ready")
        wqn_ready = sem("wqn_ready")
        nvd_ready = sem("nvd_ready")
        null_ps = sem("null_ps")
        null_sb = sem("null_sb")
        ctx_cur_ready = sem("ctx_cur_ready")
        proj_q = sem("proj_q")
        proj_k = sem("proj_k")
        proj_v = sem("proj_v")
        q_sb = sem("q_sb")
        k_lo = sem("k_lo")
        k_hi = sem("k_hi")
        v_ready = sem("v_ready")
        scored = sem("scored")
        row_max = sem("row_max")
        nmax_ready = sem("nmax_ready")
        diff_ready = sem("diff_ready")
        exp_done = sem("exp_done")
        null_exp_done = sem("null_exp_done")
        denom_ready = sem("denom_ready")
        recip_ready = sem("recip_ready")
        probs_ready = sem("probs_ready")
        null_p_ready = sem("null_p_ready")
        probs_turned = sem("probs_turned")
        pT_lo = sem("pT_lo")
        pT_hi = sem("pT_hi")
        weighed = sem("weighed")
        oT_ready = sem("oT_ready")
        out_added = sem("out_added")
        null_turned = sem("null_turned")
        null_pT_ready = sem("null_pT_ready")
        acc_done = sem("acc_done")
        acc_free = sem("acc_free")
        h2_ready = sem("h2_ready")
        logits_ps = sem("logits_ps")
        df_ready = sem("df_ready")
        ex_ready = sem("ex_ready")
        onehot_ready = sem("onehot_ready")
        prefix_ps = sem("prefix_ps")
        routed = sem("routed")
        xs_turned = [sem(f"xs_turned{j}") for j in range(2)]
        xsT_ready = [sem(f"xsT_ready{j}") for j in range(2)]
        h_ps = [sem(f"h_ps{j}") for j in range(2)]
        h_sb = [sem(f"h_sb{j}") for j in range(2)]
        y_ps = [sem(f"y_ps{j}") for j in range(2)]
        b1_ready = [sem(f"b1_ready{j}") for j in range(2)]
        y_ready = [sem(f"y_ready{j}") for j in range(2)]
        summed = [sem(f"summed{j}") for j in range(4)]

        class Link:
            n = 0

            def __call__(self, eng, ins):
                self.n += 1
                ins.then_inc(dve_chain, 1)
                eng.wait_ge(dve_chain, self.n)

        def row_of(v, parts=P):
            return v.rearrange("(a n) -> a n", a=1).partition_broadcast(parts)

        def over(ap, axis, n):
            shape = list(ap.shape)
            shape.insert(axis, n)
            return ap.unsqueeze(axis).broadcast_to(shape)

        N_SMALL = 10
        block = ctx.enter_context(nc.Block())

        @block.sync
        def _(sp):
            def group(src, g):
                return src.rearrange("b p d -> p b d")[:, g * GT:(g + 1) * GT, :]

            sp.dma_start(x_sb[:, 0:GT, :], group(x, 0)).then_inc(x_in[0], 16)
            sp.dma_start(ctx_sb[:, 0:GT, :], group(ctx_in, 0)).then_inc(c_in[0], 16)
            sp.dma_start(wq_sb, w_q.rearrange("(k p) n -> p k n", p=P)).then_inc(wq_in, 16)
            sp.dma_start(wkv_sb[0:CC], w_kv.rearrange("(c p) n -> p c n", p=CC)).then_inc(wkv_in, 16)
            for g in range(1, NG):
                sp.dma_start(x_sb[:, g * GT:(g + 1) * GT, :], group(x, g)).then_inc(x_in[g], 16)
                sp.dma_start(ctx_sb[:, g * GT:(g + 1) * GT, :], group(ctx_in, g)).then_inc(c_in[g], 16)
            sp.dma_start(wout_sb, w_out.rearrange("(c p) n -> p c n", p=P)).then_inc(wout_in, 16)
            sp.wait_ge(pool_made, 1)
            zero_view = h2_sorted.rearrange("(n p r) d -> n p (r d)", p=P, r=4)
            for n in range(NSP // 4):
                sp.dma_start(zero_view[n], zeros[:, :]).then_inc(zeroed, 16)

            sp.wait_ge(routed, 1)
            sp.wait_ge(scattered, 16 * B)
            w1_v = w_1.rearrange("e (k p) n -> e p k n", p=P)
            w2_v = w_2.rearrange("e (c p) n -> e p c n", p=P)

            def tile(i, j, reused=True):
                k = (i - 1) * 2 + j // 2
                e = sp.value_load(eid_i[0:1, ds(i * NB + j, 1)], min_val=0, max_val=E - 1)
                if reused:
                    sp.wait_ge(xs_turned[j % 2], k + 1)
                sp.dma_start(xs_sb[j], h2_sorted[ds((i * NB + j) * P, P), :]).then_inc(xs_in[j], 16)
                if reused:
                    sp.wait_ge(h_ps[j % 2], 2 * k + 2)
                sp.dma_start(w1_sb[j], w1_v[ds(e, 1)].rearrange("a p k n -> p (a k) n")).then_inc(w1_in[j], 16)
                if reused:
                    sp.wait_ge(y_ready[j % 2], k + 1)
                sp.dma_start(b2_sb[j], b_2[ds(e, 1), :].broadcast_to([P, D])).then_inc(b2_in[j], 16)
                if reused:
                    sp.wait_ge(y_ps[j % 2], k + 1)
                sp.dma_start(w2_sb[j], w2_v[ds(e, 1)].rearrange("a p c n -> p (a c) n")).then_inc(w2_in[j], 16)
                if reused:
                    store(i - 1, j)

            def store(i, j):
                sp.wait_ge(y_ready[j % 2], i * 2 + j // 2 + 1)
                sp.dma_start(y_sorted[ds((i * NB + j) * P, P), :], y_sb[j % 2]).then_inc(y_stored[j % 2], 16)

            for j in range(NB):
                tile(0, j, reused=False)
            with sp.Fori(1, NS // NB) as i:
                for j in range(NB):
                    tile(i, j)
            for j in range(NS % NB):
                tile(NS // NB, j)
            store(NS // NB - 1, NB - 1)
            for j in range(NS % NB):
                store(NS // NB, j)

            out_v = out.rearrange("b p d -> p b d")
            for q in range(4):
                sp.wait_ge(summed[q], 4)
                sp.dma_start(out_v[:, 4 * q:4 * q + 4, :], xn_sb[:, 4 * q:4 * q + 4, :]).then_inc(out_stored, 16)
            sp.wait_ge(out_stored, 64)

        @block.gpsimd
        def _(pool):
            made = [0]

            def make(ins):
                made[0] += 1
                ins.then_inc(pool_made, 1)
                pool.wait_ge(pool_made, made[0])

            make(pool.memset(zeros[:, :], 0.0))
            make(pool.memset(minus_half[:, :], -0.5))
            pool.memset(as_rows[:, :], 0.0).then_inc(rows_clear, 1)
            pool.wait_ge(rows_clear, 1)
            make(pool.memset(ident[:, :], 0.0))
            make(pool.affine_select(out=ident[:, :], in_=ident[:, :], compare_op=ALU.not_equal, fill=1.0,
                                    base=0, pattern=[[-1, P]], channel_multiplier=1))
            for g in range(NG):
                pool.wait_ge(var_ready, g + 1)
                pool.tensor_tensor(rstd[:, g * GT:(g + 1) * GT], rstd[:, g * GT:(g + 1) * GT],
                                   minus_half[:, 0:GT], ALU.pow).then_inc(pow_done, 1)
                pool.wait_ge(pow_done, g + 1)
            make(pool.memset(row0_one[:, :], 0.0))
            make(pool.memset(row0_one[0:1, :], 1.0))
            make(pool.memset(mask_bias[:, :, :], 0.0))
            make(pool.memset(kT, 0.0))
            make(pool.memset(null_p[:, :], 0.0))
            make(pool.memset(nv_diag[:, :, :], 0.0))
            for half in range(2):
                v = nv_diag[half * DH:(half + 1) * DH].rearrange("p c (b h) -> p c b h", h=H)
                make(pool.affine_select(out=v, in_=v, compare_op=ALU.not_equal, fill=1.0, base=-half,
                                        pattern=[[-2, HP], [0, P // H], [1, H]], channel_multiplier=0))
            make(pool.memset(rows_of[:, :], 1.0))
            make(pool.affine_select(out=rows_of[:, :], in_=rows_of[:, :], compare_op=ALU.is_ge, fill=0.0,
                                    base=0, pattern=[[-H, GT]], channel_multiplier=1))
            make(pool.affine_select(out=rows_of[:, :], in_=rows_of[:, :], compare_op=ALU.is_ge, fill=0.0,
                                    base=H - 1, pattern=[[H, GT]], channel_multiplier=-1))
            make(pool.memset(ones_bf[:, :], 1.0))
            make(pool.memset(before[:, :], 1.0))
            make(pool.affine_select(out=before[:, :], in_=before[:, :], compare_op=ALU.is_ge, fill=0.0,
                                    base=-1, pattern=[[1, P]], channel_multiplier=-1))
            make(pool.iota(iota_i[:, :], [[1, NS]], base=0, channel_multiplier=0))
            make(pool.memset(ones_e[:, :], 1.0))
            make(pool.memset(keep_scan[:, :, :], 1.0))
            make(pool.memset(keep_scan[:, :, 0:1], 0.0))
            pool.wait_ge(copied_act, 2 * NG)
            pool.wait_ge(copied_dve, 2 * NG)
            pool.tensor_copy(ctx_cur[0:CC], ctxT[0:CC, :, 0:GT * P]).then_inc(ctx_cur_ready, 1)
            with pool.Fori(1, NG) as g:
                pool.wait_ge(ctx_cur_ready, g)
                pool.wait_ge(proj_v, g * HP)
                pool.tensor_copy(ctx_cur[0:CC], ctxT[0:CC, :, ds(g * (GT * P), GT * P)]).then_inc(ctx_cur_ready, 1)
            pool.wait_ge(ctx_cur_ready, NG)
            for n in range(2):
                pool.wait_ge(var_ready, NG + 1 + n)
                pool.tensor_tensor(rstd[:, :], rstd[:, :], minus_half[:, :], ALU.pow).then_inc(pow_done, 1)
                pool.wait_ge(pow_done, NG + 1 + n)
            pool.wait_ge(routed, 1)
            pool.wait_ge(zeroed, 16 * (NSP // 4))
            for t in range(B):
                pool.indirect_dma_start(
                    out=h2_sorted, out_offset=bass.IndirectOffsetOnAxis(ap=pos_i[:, t:t + 1], axis=0),
                    in_=xn_sb[:, t, :], in_offset=None).then_inc(scattered, 16)

            pool.wait_ge(y_stored[0], 16 * ((NS + 1) // 2))
            pool.wait_ge(y_stored[1], 16 * (NS // 2))
            for t in range(B):
                pool.indirect_dma_start(
                    out=att_sb[:, t, :], out_offset=None,
                    in_=y_sorted, in_offset=bass.IndirectOffsetOnAxis(ap=pos_i[:, t:t + 1], axis=0),
                ).then_inc(gathered[t // 4], 16)

        @block.tensor
        def _(pe):
            for made_by_me in (probs_turned, weighed, out_added, null_turned):
                pe.sem_inc(made_by_me, CREDIT)
            pe.wait_ge(pool_made, 4)
            pe.wait_ge(small_in, 16 * N_SMALL)
            pe.transpose(banks[7][:, 0:P], as_rows[:, :], ident[:, :]).then_inc(cols_ps, 1)
            for g in range(NG):
                pe.wait_ge(xn_ready, g + 1)
                pe.wait_ge(c_in[g], 16)
                for j in range(4):
                    n = 4 * g + j
                    if n == 7:
                        pe.wait_ge(cols_ready, 1)
                    if n >= 8:
                        pe.wait_ge(copied_dve if n % 2 else copied_act, (n - 8) // 2 + 1)
                    for b in range(GT):
                        t = g * GT + b
                        if j < KD:
                            ins = pe.transpose(banks[n % 8][:, b * P:(b + 1) * P],
                                               xn_sb[:, t, j * P:(j + 1) * P], ident[:, :])
                        else:
                            ins = pe.transpose(banks[n % 8][0:CC, b * P:(b + 1) * P],
                                               ctx_sb[:, t, (j - 2) * CC:(j - 1) * CC], ident[:, :])
                    ins.then_inc(turned, 1)
            pe.wait_ge(wqn_ready, 1)
            pe.wait_ge(copied_act, 2 * NG)
            pe.wait_ge(copied_dve, 2 * NG)
            for t in range(B):
                for k in range(KD):
                    ins = pe.matmul(ps_o[:, t * H:(t + 1) * H], xT[:, k, t * P:(t + 1) * P], wqn[:, k, :],
                                    start=(k == 0), stop=(k == KD - 1))
            ins.then_inc(null_ps, 1)
            pe.wait_ge(nvd_ready, 1)
            pe.wait_ge(wout_in, 16)
            for c in range(HP):
                ins = pe.matmul(ps_acc[:, 0:D], nv_diag[:, c, :], wout_sb[:, c, :],
                                start=(c == 0), stop=(c == HP - 1))
            ins.then_inc(null_ps, 1)
            pe.wait_ge(wq_in, 16)
            pe.wait_ge(wkv_in, 16)

            def project(g, hp, first_unit=False):
                n = g * HP + hp
                tok = ds(g * (GT * P), GT * P)
                if not first_unit:
                    pe.wait_ge(q_sb, n)
                for k in range(KD):
                    ins = pe.matmul(ps_q[:, :], wq_sb[:, k, hp * P:(hp + 1) * P], xT[:, k, tok],
                                    start=(k == 0), stop=(k == KD - 1))
                ins.then_inc(proj_q, 1)
                if not first_unit:
                    pe.wait_ge(k_lo, n)
                    pe.wait_ge(k_hi, n)
                for c in range(2):
                    ins = pe.matmul(ps_k[:, :], wkv_sb[0:CC, c, hp * P:(hp + 1) * P], ctxT[0:CC, c, tok],
                                    start=(c == 0), stop=(c == 1))
                ins.then_inc(proj_k, 1)
                if not first_unit:
                    pe.wait_ge(v_ready, n)
                if hp == 0:
                    pe.wait_ge(ctx_cur_ready, g + 1)
                for b in range(GT):
                    for c in range(2):
                        ins = pe.matmul(ps_v[:, b * P:(b + 1) * P], ctx_cur[0:CC, c, b * P:(b + 1) * P],
                                        wkv_sb[0:CC, c, INNER + hp * P:INNER + (hp + 1) * P],
                                        start=(c == 0), stop=(c == 1))
                ins.then_inc(proj_v, 1)

            def add_out(g, hp):
                pe.wait_ge(oT_ready, CREDIT + g * HP + hp + 1)
                if hp == 0:
                    pe.wait_ge(acc_free, CREDIT + g)
                for b in range(GT):
                    ins = pe.matmul(ps_acc[:, b * D:(b + 1) * D], oT[:, b * P:(b + 1) * P], wout_sb[:, hp, :],
                                    start=(hp == 0 and b % 2 == 0), stop=False, skip_group_check=True)
                ins.then_inc(out_added, 1)

            def group(g, more):
                for hp in range(HP):
                    n = g * HP + hp
                    pe.wait_ge(q_sb, n + 1)
                    pe.wait_ge(k_lo, n + 1)
                    pe.wait_ge(k_hi, n + 1)
                    pe.wait_ge(pT_lo, CREDIT + n)
                    pe.wait_ge(pT_hi, CREDIT + n)
                    for two in range(GT // 2):
                        bias = mask_bias[:, ds(g * GT + 2 * two, 2), :].unsqueeze(2).broadcast_to([P, 2, 2, P])
                        pe.matmul(ps_s[:, two * 512:(two + 1) * 512], row0_one[:, :], bias,
                                  start=True, stop=False, skip_group_check=True)
                        for b in (2 * two, 2 * two + 1):
                            ins = pe.matmul(ps_s[:, b * 2 * P:(b + 1) * 2 * P], qT[:, b * P:(b + 1) * P],
                                            kT[:, b, :], start=False, stop=True, skip_group_check=True)
                    ins.then_inc(scored, 1)
                    if hp + 1 < HP:
                        project(g, hp + 1)
                    elif more:
                        project(g + 1, 0)
                    for half in range(2):
                        pe.wait_ge(probs_ready, 2 * n + half + 1)
                        for j in range(GT * half, GT * half + GT):
                            ins = pe.transpose(ps_s[:, j * P:(j + 1) * P], probs[:, j, :], ident[:, :])
                        ins.then_inc(probs_turned, 1)
                    if hp > 0:
                        add_out(g, hp - 1)
                    pe.wait_ge(v_ready, n + 1)
                    pe.wait_ge(oT_ready, CREDIT + n)
                    if hp == 0:
                        pe.wait_ge(null_pT_ready, CREDIT + g)
                    for b in range(GT):
                        if b == 0:
                            pe.wait_ge(pT_lo, CREDIT + n + 1)
                        if b == GT // 2:
                            pe.wait_ge(pT_hi, CREDIT + n + 1)
                        for h in range(2):
                            ins = pe.matmul(ps_o[h * DH:(h + 1) * DH, b * P:(b + 1) * P],
                                            v_sb[hp % 2][:, b, h * DH:(h + 1) * DH], probsT[:, 2 * b + h, :],
                                            start=True, stop=True, skip_group_check=True)
                    ins.then_inc(weighed, 1)
                pe.wait_ge(oT_ready, CREDIT + g * HP + HP)
                pe.wait_ge(null_p_ready, g * HP + HP)
                pe.transpose(ps_o[:, 0:P], null_p[:, :], ident[:, :]).then_inc(null_turned, 1)
                add_out(g, HP - 1)
                pe.wait_ge(null_pT_ready, CREDIT + g + 1)
                for b in range(GT):
                    ins = pe.matmul(ps_acc[:, b * D:(b + 1) * D], null_pT[:, :], nw_rows[:, b, :],
                                    start=False, stop=True, skip_group_check=True)
                ins.then_inc(acc_done, 1)

            pe.wait_ge(null_sb, 2)
            pe.wait_ge(mask_ready, 1)
            pe.wait_ge(pool_made, 9)
            project(0, 0, first_unit=True)
            with pe.Fori(0, NG - 1) as g:
                group(g, True)
            group(NG - 1, False)

            pe.wait_ge(acc_free, CREDIT + NG)
            base_n = 4 * NG
            for g in range(NG):
                pe.wait_ge(h2_ready, (g + 1) * GT)
                for j in range(KD):
                    n = KD * g + j
                    for b in range(GT):
                        ins = pe.transpose(banks[n][:, b * P:(b + 1) * P],
                                           xn_sb[:, g * GT + b, j * P:(j + 1) * P], ident[:, :])
                    ins.then_inc(turned, 1)
            pe.wait_ge(copied_act, 2 * NG + NG)
            pe.wait_ge(copied_dve, 2 * NG + NG)
            for t in range(B):
                for k in range(KD):
                    ins = pe.matmul(ps_q[:, t * E:(t + 1) * E], xT[:, k, t * P:(t + 1) * P], wr_sb[:, k, :],
                                    start=(k == 0), stop=(k == KD - 1))
            ins.then_inc(logits_ps, 1)
            pe.wait_ge(onehot_ready, 1)
            pe.matmul(ps_k[:, 0:B * E], before[:, :], onehot[:, :, :], start=True, stop=True)
            pe.matmul(ps_k[:, B * E:2 * B * E], ones_bf[:, :], onehot[:, :, :].rearrange("p t e -> p e t"),
                      start=True, stop=True).then_inc(prefix_ps, 1)
            pe.wait_ge(routed, 1)

            ps_h = [ps_s, ps_acc]
            ps_y = [ps_q, ps_k]
            ps_x = [ps_v, ps_o]

            def turn_rows(i, j, k):
                par = j % 2
                pe.wait_ge(xs_in[j], 16 * (i + 1))
                pe.wait_ge(xsT_ready[par], k)
                for c in range(KD):
                    ins = pe.transpose(ps_x[par][:, c * P:(c + 1) * P], xs_sb[j][:, c * P:(c + 1) * P], ident[:, :])
                ins.then_inc(xs_turned[par], 1)

            def tile(i, j, last=False):
                par, k = j % 2, i * 2 + j // 2
                pe.wait_ge(w1_in[j], 16 * (i + 1))
                pe.wait_ge(xsT_ready[par], k + 1)
                pe.wait_ge(h_sb[par], FC * k)
                for f in range(FC):
                    for c in range(KD):
                        ins = pe.matmul(ps_h[par][:, f * P:(f + 1) * P], w1_sb[j][:, c, f * P:(f + 1) * P],
                                        xsT[par][:, c, :], start=(c == 0), stop=(c == KD - 1))
                    if f % 4 == 3:
                        ins.then_inc(h_ps[par], 1)
                if not last and j + 1 < NB:
                    turn_rows(i, j + 1, i * 2 + (j + 1) // 2)
                elif not last:
                    turn_rows(i + 1, 0, i * 2 + 2)
                pe.wait_ge(w2_in[j], 16 * (i + 1))
                pe.wait_ge(y_ready[par], k)
                for f in range(FC):
                    pe.wait_ge(h_sb[par], FC * k + f + 1)
                    ins = pe.matmul(ps_y[par][:, 0:D], hT[par][:, f, :], w2_sb[j][:, f, :],
                                    start=(f == 0), stop=(f == FC - 1))
                ins.then_inc(y_ps[par], 1)

            turn_rows(0, 0, 0)
            for j in range(NB):
                tile(0, j)
            with pe.Fori(1, NS // NB) as i:
                for j in range(NB):
                    tile(i, j)
            for j in range(NS % NB):
                tile(NS // NB, j, last=(j == NS % NB - 1))

        @block.scalar
        def _(act):
            for made_by_me in (pT_lo, oT_ready, null_pT_ready, exp_done):
                act.sem_inc(made_by_me, CREDIT)
            act.dma_start(gates[:, 0:1], row_of(g_xattn)).then_inc(small_in, 16)
            act.dma_start(gates[:, 1:2], row_of(g_ffn)).then_inc(small_in, 16)
            act.dma_start(nk_row[:, :], null_kv[0:1, :].broadcast_to([P, DH])).then_inc(small_in, 16)
            act.dma_start(mask_u8[:, :], mask.rearrange("b n -> (b n)").rearrange("(a n) -> a n", a=1)
                          ).then_inc(small_in, 16)
            act.dma_start(gout_row[:, :], row_of(g_out)).then_inc(small_in, 16)
            act.dma_start(wr_sb[:, :, :], w_r.rearrange("(k p) e -> p k e", p=P)).then_inc(small_in, 16)
            act.wait_ge(rows_clear, 1)
            act.dma_start(as_rows[E * FC:E * FC + KD, :], g_norm.rearrange("(k p) -> k p", p=P)).then_inc(small_in, 16)
            for half in range(2):
                act.dma_start(as_rows[E * FC + KD:E * FC + KD + 1, half * DH:(half + 1) * DH],
                              null_kv[1:2, :]).then_inc(small_in, 16)
            act.dma_start(as_rows[0:E * FC, :], b_1.rearrange("e (c p) -> (e c) p", p=P)).then_inc(small_in, 16)
            act.wait_ge(small_in, 16 * N_SMALL)
            act.activation(tanhs[:, :], gates[:, :], ACT.Tanh).then_inc(act_setup, 1)
            act.wait_ge(cols_ps, 1)
            act.activation(as_cols[:, :], banks[7][:, 0:P], ACT.Copy).then_inc(cols_ready, 1)
            act.wait_ge(cols_ready, 1)
            for g in range(NG):
                for j in (0, 2):
                    n = 4 * g + j
                    act.wait_ge(turned, n + 1)
                    if j == 0:
                        ins = act.activation(xT[:, 0, g * GT * P:(g + 1) * GT * P], banks[n % 8], ACT.Copy,
                                             scale=gn_col[:, 0:1])
                    else:
                        ins = act.activation(ctxT[0:CC, 0, g * GT * P:(g + 1) * GT * P], banks[n % 8][0:CC],
                                             ACT.Copy)
                    ins.then_inc(copied_act, 1)

            def take_qk(n):
                act.wait_ge(proj_q, n + 1)
                act.wait_ge(scored, n)
                act.activation(qT, ps_q[:, :], ACT.Copy).then_inc(q_sb, 1)
                act.wait_ge(proj_k, n + 1)
                act.activation(kT[0:DH, :, 0:P], ps_k[0:DH, :].rearrange("p (b n) -> p b n", b=GT),
                               ACT.Copy).then_inc(k_lo, 1)

            def group(g, more):
                for hp in range(HP):
                    n = g * HP + hp
                    act.wait_ge(diff_ready, n + 1)
                    act.activation(null_exp[:, :, :], null_diff[:, :, :], ACT.Exp).then_inc(null_exp_done, 1)
                    act.wait_ge(nmax_ready, n + 1)
                    act.wait_ge(probs_turned, CREDIT + 2 * n)
                    for j in range(2 * GT):
                        ins = act.activation(probs[:, j, :], ps_s[:, j * P:(j + 1) * P], ACT.Exp,
                                             bias=nmax[:, j // 2, j % 2:j % 2 + 1], scale=SCALE,
                                             accum_out=sums[:, j // 2, j % 2:j % 2 + 1])
                    ins.then_inc(exp_done, 1)
                    if hp + 1 < HP or more:
                        take_qk(n + 1)
                    act.wait_ge(probs_turned, CREDIT + 2 * n + 1)
                    act.wait_ge(weighed, CREDIT + n)
                    act.activation(probsT[:, 0:GT, :], ps_s[:, 0:512].rearrange("p (j n) -> p j n", j=GT),
                                   ACT.Copy).then_inc(pT_lo, 1)
                    act.wait_ge(weighed, CREDIT + n + 1)
                    act.wait_ge(out_added, CREDIT + n)
                    act.activation(oT, ps_o[:, :], ACT.Copy).then_inc(oT_ready, 1)
                act.wait_ge(null_turned, CREDIT + g + 1)
                act.activation(null_pT[:, :], ps_o[:, 0:P], ACT.Copy).then_inc(null_pT_ready, 1)

            take_qk(0)
            with act.Fori(0, NG - 1) as g:
                group(g, True)
            group(NG - 1, False)

            for g in range(NG):
                act.wait_ge(turned, 4 * NG + KD * g + 1)
                act.activation(xT[:, 0, g * GT * P:(g + 1) * GT * P], banks[KD * g], ACT.Copy).then_inc(copied_act, 1)
            act.wait_ge(df_ready, 1)
            act.activation(r_b[:, :, :], r_a[:, :, :], ACT.Exp).then_inc(ex_ready, 1)

            ps_h = [ps_s, ps_acc]

            def tile(i, j):
                par, k = j % 2, i * 2 + j // 2
                act.wait_ge(b1_ready[par], k + 1)
                act.wait_ge(y_ps[par], k)
                for f in range(FC):
                    if f % 4 == 0:
                        act.wait_ge(h_ps[par], 2 * k + f // 4 + 1)
                    act.activation(hT[par][:, f, :], ps_h[par][:, f * P:(f + 1) * P], ACT.Gelu,
                                   bias=b1_cur[par][:, f:f + 1]).then_inc(h_sb[par], 1)

            for j in range(NB):
                tile(0, j)
            with act.Fori(1, NS // NB) as i:
                for j in range(NB):
                    tile(i, j)
            for j in range(NS % NB):
                tile(NS // NB, j)

        @block.vector
        def _(dve):
            for made_by_me in (pT_hi, acc_free):
                dve.sem_inc(made_by_me, CREDIT)
            link = Link()
            all_b = range(B)

            def statistics(src, tiles, scale, shift):
                for t in tiles:
                    ins = dve.bn_stats(stats[:, t, :], src[:, t, :])
                link(dve, ins)
                for t in tiles:
                    ins = dve.bn_aggr(mv[:, t, :], stats[:, t, :])
                link(dve, ins)
                a, b = tiles[0], tiles[-1] + 1
                dve.tensor_scalar(rstd[:, a:b], mv[:, a:b, 1], scale, shift, ALU.mult, ALU.add).then_inc(var_ready, 1)

            def stats_x(g):
                dve.wait_ge(x_in[g], 16)
                statistics(x_sb, range(g * GT, (g + 1) * GT), 1.0 + EPS, EPS * EPS)

            def norm_x(g):
                dve.wait_ge(pow_done, g + 1)
                for t in range(g * GT, (g + 1) * GT):
                    ins = dve.tensor_scalar(xn_sb[:, t, :], x_sb[:, t, :], mv[:, t, 0:1], rstd[:, t:t + 1],
                                            ALU.subtract, ALU.mult)
                ins.then_inc(xn_ready, 1)

            stats_x(0)
            for g in range(NG):
                if g + 1 < NG:
                    stats_x(g + 1)
                norm_x(g)
            dve.wait_ge(small_in, 16 * N_SMALL)
            dve.wait_ge(cols_ready, 1)
            for g in range(NG):
                for j in (1, 3):
                    n = 4 * g + j
                    dve.wait_ge(turned, n + 1)
                    if j == 1:
                        ins = dve.tensor_scalar(xT[:, 1, g * GT * P:(g + 1) * GT * P], banks[n % 8],
                                                gn_col[:, 1:2], None, ALU.mult)
                    else:
                        ins = dve.tensor_copy(ctxT[0:CC, 1, g * GT * P:(g + 1) * GT * P], banks[n % 8][0:CC])
                    ins.then_inc(copied_dve, 1)
            dve.wait_ge(wq_in, 16)
            by_head = wq_sb.rearrange("p k (h d) -> p (k h) d", h=H)
            nk_prod = wq_nk.rearrange("p a b -> p (a b)").rearrange("p (m d) -> p m d", d=DH)
            link(dve, dve.tensor_tensor(nk_prod, by_head, over(nk_row[:, :], 1, KD * H), ALU.mult))
            dve.tensor_reduce(wqn[:, :, :].rearrange("p k h -> p (k h)"), nk_prod, AX_X, ALU.add).then_inc(wqn_ready, 1)
            dve.wait_ge(pool_made, 15)
            dve.tensor_scalar(nv_diag[:, :, :], nv_diag[:, :, :], nv_col[:, 0:1], None, ALU.mult).then_inc(nvd_ready, 1)
            dve.tensor_scalar(mask_bias[0:1, :, :].rearrange("p b n -> p (b n)"), mask_u8[:, :], -1.0, MASKED,
                              ALU.add, ALU.mult).then_inc(mask_ready, 1)
            dve.wait_ge(act_setup, 1)
            link(dve, dve.tensor_scalar(gout_row[:, :], gout_row[:, :], tanhs[:, 0:1], None, ALU.mult))
            dve.wait_ge(null_ps, 1)
            dve.tensor_scalar(nsn[:, :, :].rearrange("p b h -> p (b h)"), ps_o[:, 0:B * H], -SCALE, None,
                              ALU.mult).then_inc(null_sb, 1)
            dve.wait_ge(null_ps, 2)
            for b in range(GT):
                ins = dve.tensor_scalar(nw_rows[:, b, :], ps_acc[:, 0:D], rows_of[:, b:b + 1], None, ALU.mult)
            ins.then_inc(null_sb, 1)
            dve.wait_ge(null_sb, 2)

            def take_k(n):
                dve.wait_ge(proj_k, n + 1)
                dve.wait_ge(scored, n)
                dve.tensor_copy(kT[DH:P, :, P:2 * P], ps_k[DH:P, :].rearrange("p (b n) -> p b n", b=GT)
                                ).then_inc(k_hi, 1)

            def take_v(n, par, first_unit=False):
                dve.wait_ge(proj_v, n + 1)
                if not first_unit:
                    dve.wait_ge(weighed, CREDIT + n - 1)
                dve.tensor_copy(v_sb[par], ps_v[:, :].rearrange("p (b n) -> p b n", b=GT)).then_inc(v_ready, 1)

            def group(g, more):
                for hp in range(HP):
                    n = g * HP + hp
                    pair = slice(2 * hp, 2 * hp + 2)
                    dve.wait_ge(scored, n + 1)
                    dve.wait_ge(exp_done, CREDIT + n)
                    dve.tensor_reduce(rowmax[:, :, :].rearrange("p b h -> p (b h)"),
                                      ps_s[:, :].rearrange("p (j n) -> p j n", n=P), AX_X, ALU.max
                                      ).then_inc(row_max, 1)
                    dve.wait_ge(row_max, n + 1)
                    null = nsn[:, ds(g * GT, GT), pair]
                    dve.scalar_tensor_tensor(out=nmax[:, :, :], in0=rowmax[:, :, :], scalar=-SCALE, in1=null,
                                             op0=ALU.mult, op1=ALU.min).then_inc(nmax_ready, 1)
                    dve.wait_ge(nmax_ready, n + 1)
                    dve.tensor_tensor(null_diff[:, :, :], nmax[:, :, :], null, ALU.subtract).then_inc(diff_ready, 1)
                    if hp + 1 < HP or more:
                        take_k(n + 1)
                    dve.wait_ge(null_exp_done, n + 1)
                    dve.wait_ge(exp_done, CREDIT + n + 1)
                    dve.tensor_tensor(denom[:, :, :], sums[:, :, :], null_exp[:, :, :], ALU.add
                                      ).then_inc(denom_ready, 1)
                    dve.wait_ge(denom_ready, n + 1)
                    dve.reciprocal(recip[:, :, :], denom[:, :, :]).then_inc(recip_ready, 1)
                    dve.wait_ge(recip_ready, n + 1)
                    for half in range(2):
                        part = probs[:, half * GT:(half + 1) * GT, :]
                        by = recip[:, 2 * half:2 * half + 2, :].rearrange("p b h -> p (b h)")
                        dve.tensor_tensor(part, part, over(by, 2, P), ALU.mult).then_inc(probs_ready, 1)
                    if hp == 0:
                        dve.wait_ge(null_turned, CREDIT + g)
                    dve.tensor_tensor(null_p[:, 0:GT * H].rearrange("p (b h) -> p b h", h=H)[:, :, pair],
                                      null_exp[:, :, :], recip[:, :, :], ALU.mult).then_inc(null_p_ready, 1)
                    if hp + 1 < HP or more:
                        take_v(n + 1, (hp + 1) % 2)
                    dve.wait_ge(probs_turned, CREDIT + 2 * n + 2)
                    dve.wait_ge(weighed, CREDIT + n)
                    dve.tensor_copy(probsT[:, GT:2 * GT, :], ps_s[:, 512:1024].rearrange("p (j n) -> p j n", j=GT)
                                    ).then_inc(pT_hi, 1)
                dve.wait_ge(acc_done, g + 1)
                dve.tensor_copy(att_sb[:, ds(g * GT, GT), :], ps_acc[:, :].rearrange("p (b n) -> p b n", b=GT)
                                ).then_inc(acc_free, 1)

            take_k(0)
            take_v(0, 0, first_unit=True)
            with dve.Fori(0, NG - 1) as g:
                group(g, True)
            group(NG - 1, False)

            dve.wait_ge(acc_free, CREDIT + NG)
            statistics(att_sb, all_b, 1.0, EPS)
            for t in all_b:
                ins = dve.scalar_tensor_tensor(out=att_sb[:, t, :], in0=att_sb[:, t, :], scalar=mv[:, t, 0:1],
                                               in1=gout_row[:, :], op0=ALU.subtract, op1=ALU.mult)
            link(dve, ins)
            dve.wait_ge(pow_done, NG + 1)
            for t in all_b:
                ins = dve.scalar_tensor_tensor(out=x_sb[:, t, :], in0=att_sb[:, t, :], scalar=rstd[:, t:t + 1],
                                               in1=x_sb[:, t, :], op0=ALU.mult, op1=ALU.add)
            link(dve, ins)
            statistics(x_sb, all_b, 1.0, EPS)
            dve.wait_ge(pow_done, NG + 2)
            for t in all_b:
                dve.tensor_scalar(xn_sb[:, t, :], x_sb[:, t, :], mv[:, t, 0:1], rstd[:, t:t + 1],
                                  ALU.subtract, ALU.mult).then_inc(h2_ready, 1)
            for g in range(NG):
                dve.wait_ge(turned, 4 * NG + KD * g + 2)
                dve.tensor_copy(xT[:, 1, g * GT * P:(g + 1) * GT * P], banks[KD * g + 1]).then_inc(copied_dve, 1)

            dve.wait_ge(logits_ps, 1)
            flat = "p t e -> p (t e)"
            link(dve, dve.tensor_copy(logits[:, :, :].rearrange(flat), ps_q[:, 0:B * E]))
            link(dve, dve.tensor_reduce(r_max[:, :], logits[:, :, :], AX_X, ALU.max))
            dve.tensor_tensor(r_a[:, :, :], logits[:, :, :], over(r_max[:, :], 2, E), ALU.subtract).then_inc(df_ready, 1)
            dve.wait_ge(pool_made, 22)
            link(dve, dve.tensor_copy(iota_s[:, :], iota_i[:, :]))
            link(dve, dve.tensor_scalar(iota_e8[:, :], iota_s[:, 0:E], float(-E), None, ALU.add))
            link(dve, dve.tensor_tensor(past[:, 0:B, :], logits[:, :, :], over(r_max[:, :], 2, E), ALU.is_equal))
            link(dve, dve.tensor_tensor(logits[:, :, :], past[:, 0:B, :], over(iota_e8[:, :], 1, B), ALU.mult))
            link(dve, dve.tensor_reduce(first[:, :], logits[:, :, :], AX_X, ALU.min))
            dve.tensor_tensor(onehot[:, :, :], over(iota_e8[:, :], 1, B), over(first[:, :], 2, E),
                              ALU.is_equal).then_inc(onehot_ready, 1)
            dve.wait_ge(ex_ready, 1)
            link(dve, dve.tensor_reduce(r_sum[:, :], r_b[:, :, :], AX_X, ALU.add))
            link(dve, dve.reciprocal(coef[:, :], r_sum[:, :]))
            link(dve, dve.tensor_scalar(coef[:, :], coef[:, :], tanhs[:, 1:2], None, ALU.mult))
            dve.wait_ge(prefix_ps, 1)
            link(dve, dve.tensor_copy(counts[:, :, :].rearrange("p e t -> p (e t)"), ps_k[:, B * E:2 * B * E]))
            link(dve, dve.tensor_tensor_scan(upto[:, :, :].rearrange("p e t -> p (e t)"),
                                             keep_scan[:, :, :].rearrange("p e t -> p (e t)"),
                                             counts[:, :, :].rearrange("p e t -> p (e t)"), 0.0,
                                             ALU.mult, ALU.add))
            link(dve, dve.tensor_scalar(tiles_i[:, :], upto[:, :, B - 1], float(P - 1), None, ALU.add))
            link(dve, dve.tensor_scalar(tiles_i[:, :], tiles_i[:, :], P.bit_length() - 1, None, ALU.logical_shift_right))
            link(dve, dve.tensor_copy(tiles_n[:, :], tiles_i[:, :]))
            link(dve, dve.tensor_tensor_scan(ends[:, :], ones_e[:, :], tiles_n[:, :], 0.0, ALU.mult, ALU.add))
            link(dve, dve.tensor_tensor(starts[:, :], ends[:, :], tiles_n[:, :], ALU.subtract))
            link(dve, dve.tensor_tensor(base[:, :, :], upto[:, :, :], counts[:, :, :], ALU.subtract))
            link(dve, dve.scalar_tensor_tensor(out=base[:, :, :], in0=over(starts[:, :], 2, B), scalar=float(P),
                                               in1=base[:, :, :], op0=ALU.mult, op1=ALU.add))
            link(dve, dve.tensor_tensor(r_a[:, :, :], ps_k[:, 0:B * E].rearrange("p (t e) -> p t e", e=E),
                                        base[:, :, :].rearrange("p e t -> p t e"), ALU.add))
            link(dve, dve.tensor_tensor(r_a[:, :, :], r_a[:, :, :], onehot[:, :, :], ALU.mult))
            link(dve, dve.tensor_reduce(pos_f[:, :], r_a[:, :, :], AX_X, ALU.add))
            link(dve, dve.tensor_copy(pos_i[:, :], pos_f[:, :]))
            link(dve, dve.tensor_tensor(past[:, :, :], over(ends[:, :], 1, NS), over(iota_s[:, :], 2, E), ALU.is_le))
            link(dve, dve.tensor_reduce(eid_f[:, :], past[:, :, :], AX_X, ALU.add))
            link(dve, dve.tensor_scalar(eid_f[:, :], eid_f[:, :], float(E - 1), None, ALU.min))
            dve.tensor_copy(eid_i[:, :], eid_f[:, :]).then_inc(routed, 1)
            dve.wait_ge(routed, 1)

            ps_y = [ps_q, ps_k]
            ps_x = [ps_v, ps_o]

            def take_rows(par, k):
                dve.wait_ge(xs_turned[par], k + 1)
                dve.wait_ge(h_ps[par], 2 * k)
                dve.tensor_copy(xsT[par], ps_x[par][:, 0:KD * P].rearrange("p (k n) -> p k n", k=KD)
                                ).then_inc(xsT_ready[par], 1)

            def tile(i, j, last=False):
                par, k = j % 2, i * 2 + j // 2
                e = dve.value_load(eid_i[0:1, ds(i * NB + j, 1)], min_val=0, max_val=E - 1)
                dve.wait_ge(h_sb[par], FC * k)
                dve.tensor_copy(b1_cur[par], b1T[:, ds(e * FC, FC)]).then_inc(b1_ready[par], 1)
                if not last:
                    take_rows((j + 1) % 2, i * 2 + (j + 1) // 2)
                dve.wait_ge(y_ps[par], k + 1)
                dve.wait_ge(b2_in[j], 16 * (i + 1))
                dve.wait_ge(y_stored[par], 16 * k)
                dve.tensor_tensor(y_sb[par], ps_y[par][:, 0:D], b2_sb[j], ALU.add).then_inc(y_ready[par], 1)

            take_rows(0, 0)
            for j in range(NB):
                tile(0, j)
            with dve.Fori(1, NS // NB) as i:
                for j in range(NB):
                    tile(i, j)
            for j in range(NS % NB):
                tile(NS // NB, j, last=(j == NS % NB - 1))

            for t in all_b:
                if t % 4 == 0:
                    dve.wait_ge(gathered[t // 4], 64)
                dve.scalar_tensor_tensor(out=xn_sb[:, t, :], in0=att_sb[:, t, :], scalar=coef[:, t:t + 1],
                                         in1=x_sb[:, t, :], op0=ALU.mult, op1=ALU.add).then_inc(summed[t // 4], 1)


_INS = ['x', 'ctx_768', 'mask_BxS2_bf1', 'g_xattn', 'g_ffn', 'L0_xattn_g_norm', 'L0_xattn_null_kv',
        'L0_xattn_Wq', 'L0_xattn_Wkv', 'L0_xattn_Wout', 'L0_xattn_g_out', 'L0_ffn_Wr', 'L0_ffn_W1',
        'L0_ffn_b1', 'L0_ffn_W2', 'L0_ffn_b2']
_OUTS = [((16, 128, 256), 'float32')]


def kernel(**inputs):
    import numpy as _np
    import concourse.bacc as _bacc
    from concourse import mybir as _mybir
    from concourse.bass_utils import run_bass_kernel_spmd as _run

    nc = _bacc.Bacc("TRN2", target_bir_lowering=False, num_devices=1)
    arrays, args = {}, []
    for name in _INS:
        a = _np.ascontiguousarray(inputs[name])
        if a.dtype.kind == "b":
            a = a.view(_np.uint8)
        arrays[f"in_{name}_dram"] = a
        args.append(nc.dram_tensor(f"in_{name}_dram", a.shape, _mybir.dt.from_np(a.dtype), kind="ExternalInput").ap())
    for i, (shape, dtype) in enumerate(_OUTS):
        dt = _mybir.dt.from_np(_np.dtype(dtype))
        args.append(nc.dram_tensor(f"out_{i}_dram", shape, dt, kind="ExternalOutput").ap())
    flamingo_layer(nc, *args)
    r = _run(nc, [arrays], core_ids=[0])
    got = tuple(r.results[0][f"out_{i}_dram"] for i in range(len(_OUTS)))
    return got[0]
```

```python
from contextlib import ExitStack

import concourse.bass as bass
from concourse import mybir

P = 128
ALU = mybir.AluOpType
ACT = mybir.ActivationFunctionType
F32 = mybir.dt.float32
BF16 = mybir.dt.bfloat16
I32 = mybir.dt.int32
U8 = mybir.dt.uint8
AX_X = mybir.AxisListType.X
EPS = 1e-5
MASKED = 1e30
ds = bass.ds


def flamingo_layer(nc, x, ctx_in, mask, g_xattn, g_ffn, g_norm, null_kv, w_q, w_kv, w_out,
                   g_out, w_r, w_1, b_1, w_2, b_2, out):
    B, N, D = x.shape
    C = ctx_in.shape[2]
    INNER = w_q.shape[1]
    DH = null_kv.shape[1]
    H = INNER // DH
    E, F = b_1.shape
    assert N == P and ctx_in.shape[1] == P and 2 * DH == P
    KD = D // P
    CC = C // 2
    HP = H // 2
    GT = 4
    GP = GT * P
    NG = B // GT
    SCALE = DH ** -0.5
    FC = F // P
    NS = B + E - 1
    NB = 4
    CAP = B * P + P
    FILL = E * CAP
    ROW = 2 * D + 4
    COEF, TOKEN = 2 * D, 2 * D + 1
    NO_TOKEN = 2 * B * P

    with ExitStack() as ctx:
        def sb(name, shape, dt=F32):
            return ctx.enter_context(nc.sbuf_tensor(name, shape, dt))

        def sem(name):
            return ctx.enter_context(nc.semaphore(name))

        rows_list = nc.dram_tensor("rows_list", (FILL + P, ROW), F32).ap()

        ARENA = 26624
        arena = sb("arena", [P, ARENA])
        used = [0]

        def carve(cols):
            used[0] += cols
            assert used[0] <= ARENA
            return arena[:, used[0] - cols:used[0]]

        ctx_sb = carve(GT * C).rearrange("p (b c) -> p b c", b=GT)
        xT = carve(KD * B * P).rearrange("p (k t) -> p k t", k=KD)
        ctxT = carve(2 * B * P).rearrange("p (c t) -> p c t", c=2)
        wq_sb = carve(KD * INNER).rearrange("p (k n) -> p k n", k=KD)
        wkv_sb = carve(4 * INNER).rearrange("p (c n) -> p c n", c=2)
        qT = carve(GP)
        kT = carve(GT * 2 * P).rearrange("p (b n) -> p b n", b=GT)
        v_sb = [carve(GP).rearrange("p (b n) -> p b n", b=GT) for _ in range(2)]
        probs = carve(GT * 2 * P).rearrange("p (j n) -> p j n", j=2 * GT)
        probsT = carve(GT * 2 * P).rearrange("p (j n) -> p j n", j=2 * GT)
        oT = carve(GP)
        used[0] = 0
        w1_sb = [carve(KD * F).rearrange("p (k n) -> p k n", k=KD) for _ in range(NB)]
        w2_sb = [carve(FC * D).rearrange("p (c n) -> p c n", c=FC) for _ in range(NB)]
        b2_sb = [carve(D) for _ in range(NB)]
        hT = [carve(FC * P).rearrange("p (c n) -> p c n", c=FC) for _ in range(2)]
        xs_sb = [carve(ROW) for _ in range(NB)]
        xsT = [carve(KD * P).rearrange("p (k n) -> p k n", k=KD) for _ in range(2)]
        y_sb = [carve(D) for _ in range(NB)]
        b1_cur = [carve(FC) for _ in range(2)]

        x_sb = sb("x_sb", [P, B, D])
        xn_cur = sb("xn_cur", [P, GT, D])
        ctx_cur = sb("ctx_cur", [P, 2, GP])
        xT_cur = sb("xT_cur", [P, KD, GP])
        wout_sb = sb("wout_sb", [P, HP, D])
        att_cur = sb("att_cur", [P, GT, D])
        stage = sb("stage", [P, GT, ROW])
        h2T = sb("h2T", [P, KD, GP])
        ident = sb("ident", [P, P])
        row0_one = sb("row0_one", [P, P], BF16)
        mask_u8 = sb("mask_u8", [1, B * P], U8)
        mask_bias = sb("mask_bias", [P, B, P], BF16)
        before = sb("before", [P, P], BF16)
        ones_bf = sb("ones_bf", [P, P], BF16)
        gout_row = sb("gout_row", [P, D])
        nk_row = sb("nk_row", [P, DH])
        wr_sb = sb("wr_sb", [P, KD, E])
        gates = sb("gates", [P, 2])
        tanhs = sb("tanhs", [P, 2])
        stats = sb("stats", [P, GT, 6])
        mv_x = sb("mv_x", [P, GT, 2])
        mv_a = sb("mv_a", [P, GT, 2])
        mv_h = sb("mv_h", [P, GT, 2])
        rstd_x = sb("rstd_x", [P, GT])
        rstd_a = sb("rstd_a", [P, GT])
        rstd_h = sb("rstd_h", [P, GT])
        minus_half = sb("minus_half", [P, GT])
        wqn = sb("wqn", [P, KD, H])
        nk_prod = sb("nk_prod", [P, KD * H, DH])
        nv_diag = sb("nv_diag", [P, HP, P])
        rows_of = sb("rows_of", [P, GT])
        nw_rows = sb("nw_rows", [P, GT, D])
        nsn = sb("nsn", [P, B, H])
        rowmax = sb("rowmax", [P, GT, 2])
        nmax = sb("nmax", [P, GT, 2])
        null_diff = sb("null_diff", [P, GT, 2])
        null_exp = sb("null_exp", [P, GT, 2])
        sums = sb("sums", [P, GT, 2])
        denom = sb("denom", [P, GT, 2])
        recip = sb("recip", [P, GT, 2])
        null_p = sb("null_p", [P, P])
        null_pT = sb("null_pT", [P, P])
        logits = sb("logits", [P, GT, E])
        onehot = sb("onehot", [P, GT, E], BF16)
        r_a = sb("r_a", [P, GT, E])
        r_b = sb("r_b", [P, GT, E])
        r_max = sb("r_max", [P, GT])
        r_sum = sb("r_sum", [P, GT])
        first_e = sb("first_e", [P, GT])
        token_i = sb("token_i", [P, B], I32)
        iota_i = sb("iota_i", [P, NS], I32)
        iota_s = sb("iota_s", [P, NS])
        iota_e8 = sb("iota_e8", [P, E])
        region = sb("region", [P, E])
        taken = sb("taken", [P, E])
        keep_scan = sb("keep_scan", [P, E, GT])
        counts = sb("counts", [P, E, GT])
        upto = sb("upto", [P, E, GT])
        base = sb("base", [P, E, GT])
        pos_f = sb("pos_f", [P, GT])
        pos_i = sb("pos_i", [P, GT], I32)
        total = sb("total", [P, E])
        tiles_i = sb("tiles_i", [P, E], I32)
        tiles_n = sb("tiles_n", [P, E])
        ones_e = sb("ones_e", [P, E])
        ends = sb("ends", [P, E])
        starts = sb("starts", [P, E])
        has = sb("has", [P, NS, E])
        t_a = sb("t_a", [P, NS, E])
        in_use = sb("in_use", [P, NS])
        tile_f = sb("tile_f", [P, NS])
        tile_g = sb("tile_g", [P, NS])
        eid_i = sb("eid_i", [P, NS], I32)
        row_i = sb("row_i", [P, NS], I32)
        fill_f = sb("fill_f", [P, E])
        fill_i = sb("fill_i", [P, E], I32)
        filling = sb("filling", [P, ROW])
        as_rows = sb("as_rows", [P, P])
        as_cols = sb("as_cols", [P, P])
        b1T = as_cols[:, 0:E * FC]
        gn_col = as_cols[:, E * FC:E * FC + KD]
        nv_col = as_cols[:, E * FC + KD:E * FC + KD + 1]

        ps_q = ctx.enter_context(nc.psum_tensor("ps_q", [P, 512], F32))
        ps_kv = ctx.enter_context(nc.psum_tensor("ps_kv", [P, 512], F32))
        ps_side = ctx.enter_context(nc.psum_tensor("ps_side", [P, 512], F32))
        ps_s = ctx.enter_context(nc.psum_tensor("ps_s", [P, 1024], F32))
        ps_acc = ctx.enter_context(nc.psum_tensor("ps_acc", [P, 1024], F32))
        ps_o = ctx.enter_context(nc.psum_tensor("ps_o", [P, 512], F32))

        x_in = [sem(f"x_in{g}") for g in range(NG)]
        c_in = sem("c_in")
        rows_in = sem("rows_in")
        small_in = sem("small_in")
        wq_in = sem("wq_in")
        wkv_in = sem("wkv_in")
        wout_in = sem("wout_in")
        filled = sem("filled")
        listed = sem("listed")
        w1_in = [sem(f"w1_in{j}") for j in range(NB)]
        w2_in = [sem(f"w2_in{j}") for j in range(NB)]
        b2_in = [sem(f"b2_in{j}") for j in range(NB)]
        xs_in = [sem(f"xs_in{j}") for j in range(NB)]
        sent = [sem(f"sent{j}") for j in range(NB)]
        pool_made = sem("pool_made")
        waited = sem("waited")
        xvar_ready = sem("xvar_ready")
        avar_ready = sem("avar_ready")
        hvar_ready = sem("hvar_ready")
        xpow_done = sem("xpow_done")
        apow_done = sem("apow_done")
        hpow_done = sem("hpow_done")
        dve_chain = sem("dve_chain")
        x_step = sem("x_step")
        f_step = sem("f_step")
        xn_ready = sem("xn_ready")
        turned = sem("turned")
        copied = sem("copied")
        cols_ps = sem("cols_ps")
        cols_ready = sem("cols_ready")
        act_setup = sem("act_setup")
        mask_ready = sem("mask_ready")
        wqn_ready = sem("wqn_ready")
        nvd_ready = sem("nvd_ready")
        null_ps = sem("null_ps")
        nsn_ready = sem("nsn_ready")
        nw_ps = sem("nw_ps")
        nw_ready = sem("nw_ready")
        ctxT_ready = sem("ctxT_ready")
        ctx_cur_ready = sem("ctx_cur_ready")
        xT_cur_ready = sem("xT_cur_ready")
        side_ps = sem("side_ps")
        side_free = sem("side_free")
        proj_q = sem("proj_q")
        proj_k = sem("proj_k")
        proj_v = sem("proj_v")
        q_ready = sem("q_ready")
        k_ready = sem("k_ready")
        v_ready = sem("v_ready")
        scored = sem("scored")
        row_max = sem("row_max")
        nmax_ready = sem("nmax_ready")
        diff_ready = sem("diff_ready")
        null_exp_done = sem("null_exp_done")
        exp_done = sem("exp_done")
        denom_ready = sem("denom_ready")
        recip_ready = sem("recip_ready")
        probs_ready = sem("probs_ready")
        null_p_ready = sem("null_p_ready")
        probs_turned = sem("probs_turned")
        pT_lo = sem("pT_lo")
        pT_hi = sem("pT_hi")
        weighed = sem("weighed")
        oT_ready = sem("oT_ready")
        out_added = sem("out_added")
        null_turned = sem("null_turned")
        null_pT_ready = sem("null_pT_ready")
        acc_done = sem("acc_done")
        acc_free = sem("acc_free")
        stage_free = sem("stage_free")
        h2_ready = sem("h2_ready")
        df_ready = sem("df_ready")
        ex_ready = sem("ex_ready")
        onehot_ready = sem("onehot_ready")
        placed = sem("placed")
        tables_ready = sem("tables_ready")
        xs_turned = [sem(f"xs_turned{j}") for j in range(2)]
        xsT_ready = [sem(f"xsT_ready{j}") for j in range(2)]
        h_ps = [sem(f"h_ps{j}") for j in range(2)]
        h_sb = [sem(f"h_sb{j}") for j in range(2)]
        y_ps = [sem(f"y_ps{j}") for j in range(2)]
        b1_ready = [sem(f"b1_ready{j}") for j in range(2)]
        y_added = sem("y_added")
        y_ready = [sem(f"y_ready{j}") for j in range(2)]

        def row_of(v, parts=P):
            return v.rearrange("(a n) -> a n", a=1).partition_broadcast(parts)

        def over(ap, axis, n):
            shape = list(ap.shape)
            shape.insert(axis, n)
            return ap.unsqueeze(axis).broadcast_to(shape)

        FIRST_TASKS = 5

        def task(g, hp):
            if isinstance(g, int) and g == 0:
                return min(hp, 4)
            if isinstance(g, int) and g >= NG - 1:
                return FIRST_TASKS + HP * (NG - 2) + 4 * (g - NG + 1) + hp - 4
            return (g - 1) * HP + FIRST_TASKS + hp

        N_ROWS, N_SMALL = 4, 6
        X_STEPS, F_STEPS = 2, 25
        block = ctx.enter_context(nc.Block())

        @block.sync
        def _(sp):
            def group(src, g):
                return src.rearrange("b p d -> p b d")[:, g * GT:(g + 1) * GT, :]

            sp.dma_start(x_sb[:, 0:GT, :], group(x, 0)).then_inc(x_in[0], 16)
            sp.dma_start(ctx_sb, group(ctx_in, 0)).then_inc(c_in, 16)
            sp.dma_start(wkv_sb[0:CC], w_kv.rearrange("(c p) n -> p c n", p=CC)).then_inc(wkv_in, 16)
            sp.dma_start(wq_sb, w_q.rearrange("(k p) n -> p k n", p=P)).then_inc(wq_in, 16)
            for g in range(1, NG):
                sp.dma_start(x_sb[:, g * GT:(g + 1) * GT, :], group(x, g)).then_inc(x_in[g], 16)
                if g == 1:
                    sp.wait_ge(turned, 2)
                    sp.dma_start(ctx_sb, group(ctx_in, 1)).then_inc(c_in, 16)
                    sp.dma_start(wout_sb[:, :, :], w_out.rearrange("(c p) n -> p c n", p=P)).then_inc(wout_in, 16)
            sp.wait_ge(pool_made, 19)
            sp.dma_start(rows_list[FILL:FILL + P, :], filling[:, :]).then_inc(filled, 16)

            for g in range(2, NG):
                sp.wait_ge(side_ps, task(g - 2, 1) + 1)
                sp.dma_start(ctx_sb, group(ctx_in, g)).then_inc(c_in, 16)

            w1_v = w_1.rearrange("e (k p) n -> e p k n", p=P)
            w2_v = w_2.rearrange("e (c p) n -> e p c n", p=P)

            def weights(i, j, reused=True):
                k = (i - 1) * 2 + j // 2
                e = sp.value_load(eid_i[0:1, ds(i * NB + j, 1)], min_val=0, max_val=E - 1)
                if reused:
                    sp.wait_ge(h_ps[j % 2], 2 * k + 2)
                sp.dma_start(w1_sb[j], w1_v[ds(e, 1)].rearrange("a p k n -> p (a k) n")).then_inc(w1_in[j], 16)
                if reused:
                    sp.wait_ge(y_ps[j % 2], k + 1)
                sp.dma_start(w2_sb[j], w2_v[ds(e, 1)].rearrange("a p c n -> p (a c) n")).then_inc(w2_in[j], 16)
                if reused:
                    sp.wait_ge(y_ready[j % 2], k + 1)
                sp.dma_start(b2_sb[j], b_2[ds(e, 1), :].broadcast_to([P, D])).then_inc(b2_in[j], 16)

            def rows(i, j, reused=True):
                r = sp.value_load(row_i[0:1, ds(i * NB + j, 1)], min_val=0, max_val=FILL)
                if reused:
                    sp.wait_ge(sent[j], 16 * i)
                sp.dma_start(xs_sb[j], rows_list[ds(r, P), :]).then_inc(xs_in[j], 16)

            sp.wait_ge(tables_ready, 1)
            weights(0, 0, reused=False)
            for e in range(E):
                r = sp.value_load(fill_i[0:1, e:e + 1], min_val=0, max_val=FILL - P)
                sp.dma_start(rows_list[ds(r, P), :], filling[:, :]).then_inc(filled, 16)
            sp.wait_ge(listed, 16 * B)
            sp.wait_ge(filled, 16 * (E + 1))
            rows(0, 0, reused=False)
            for j in range(1, NB):
                weights(0, j, reused=False)
                rows(0, j, reused=False)
            with sp.Fori(1, NS // NB) as i:
                for j in range(NB):
                    weights(i, j)
                    rows(i, j)
            for j in range(NS % NB):
                weights(NS // NB, j)
                rows(NS // NB, j)
            for j in range(NB):
                sp.wait_ge(sent[j], 16 * ((NS - j + NB - 1) // NB))

        @block.gpsimd
        def _(pool):
            made = [0]

            def make(ins):
                made[0] += 1
                ins.then_inc(pool_made, 1)
                pool.wait_ge(pool_made, made[0])

            def power(rstd, ready, done, n):
                pool.wait_ge(ready, n)
                pool.tensor_tensor(rstd[:, :], rstd[:, :], minus_half[:, :], ALU.pow).then_inc(done, 1)
                pool.wait_ge(done, n)

            make(pool.memset(as_rows[:, :], 0.0))
            make(pool.memset(minus_half[:, :], -0.5))
            make(pool.memset(ident[:, :], 0.0))
            make(pool.affine_select(out=ident[:, :], in_=ident[:, :], compare_op=ALU.not_equal, fill=1.0,
                                    base=0, pattern=[[-1, P]], channel_multiplier=1))
            power(rstd_x, xvar_ready, xpow_done, 1)
            make(pool.memset(kT, 0.0))
            make(pool.memset(row0_one[:, :], 0.0))
            make(pool.memset(row0_one[0:1, :], 1.0))
            make(pool.memset(mask_bias[:, :, :], 0.0))
            make(pool.memset(null_p[:, :], 0.0))
            pool.wait_ge(copied, 4)
            pool.tensor_copy(ctx_cur[0:CC], ctxT[0:CC, :, 0:GP]).then_inc(ctx_cur_ready, 1)
            pool.wait_ge(ctx_cur_ready, 1)
            make(pool.memset(nv_diag[:, :, :], 0.0))
            for half in range(2):
                v = nv_diag[half * DH:(half + 1) * DH].rearrange("p c (b h) -> p c b h", h=H)
                make(pool.affine_select(out=v, in_=v, compare_op=ALU.not_equal, fill=1.0, base=-half,
                                        pattern=[[-2, HP], [0, P // H], [1, H]], channel_multiplier=0))
            make(pool.memset(rows_of[:, :], 1.0))
            make(pool.affine_select(out=rows_of[:, :], in_=rows_of[:, :], compare_op=ALU.is_ge, fill=0.0,
                                    base=0, pattern=[[-H, GT]], channel_multiplier=1))
            make(pool.affine_select(out=rows_of[:, :], in_=rows_of[:, :], compare_op=ALU.is_ge, fill=0.0,
                                    base=H - 1, pattern=[[H, GT]], channel_multiplier=-1))
            make(pool.memset(filling[:, :], 0.0))
            make(pool.iota(token_i[:, :], [[P, B]], base=0, channel_multiplier=1))
            make(pool.memset(stage[:, :, 2 * D:ROW], 0.0))
            make(pool.iota(filling[:, TOKEN:TOKEN + 1].bitcast(I32), [[1, 1]], base=NO_TOKEN,
                           channel_multiplier=0))
            make(pool.memset(ones_bf[:, :], 1.0))
            make(pool.memset(before[:, :], 1.0))
            make(pool.affine_select(out=before[:, :], in_=before[:, :], compare_op=ALU.is_ge, fill=0.0,
                                    base=-1, pattern=[[1, P]], channel_multiplier=-1))
            make(pool.iota(iota_i[:, :], [[1, NS]], base=0, channel_multiplier=0))
            make(pool.memset(ones_e[:, :], 1.0))
            make(pool.memset(taken[:, :], 0.0))
            make(pool.memset(keep_scan[:, :, :], 1.0))
            make(pool.memset(keep_scan[:, :, 0:1], 0.0))
            pool.sem_inc(stage_free, 1)

            def next_context(g):
                pool.wait_ge(proj_v, (g + 1) * HP)
                pool.wait_ge(ctxT_ready, 2 * g + 2)
                pool.tensor_copy(ctx_cur[0:CC], ctxT[0:CC, :, ds((g + 1) * GP, GP)]).then_inc(ctx_cur_ready, 1)

            def next_x(g):
                pool.wait_ge(side_free, task(g, 3) + 1)
                pool.tensor_copy(xT_cur[:, :, :], xT[:, :, ds((g + 1) * GP, GP)]).then_inc(xT_cur_ready, 1)
                pool.wait_ge(xT_cur_ready, g + 1)

            def list_rows(last):
                pool.wait_ge(placed, last + 1)
                pool.sem_inc(waited, 1)
                for b in range(GT):
                    pool.indirect_dma_start(
                        out=rows_list, out_offset=bass.IndirectOffsetOnAxis(ap=pos_i[:, b:b + 1], axis=0),
                        in_=stage[:, b, :], in_offset=None).then_inc(listed, 16)
                pool.wait_ge(listed, 16 * GT * (last + 1))
                pool.sem_inc(stage_free, 1)

            def group(g, first=False, last=False):
                if not first:
                    power(rstd_a, avar_ready, apow_done, g)
                if not last:
                    power(rstd_x, xvar_ready, xpow_done, g + 2)
                if not first:
                    power(rstd_h, hvar_ready, hpow_done, g)
                if not last:
                    next_x(g)
                    next_context(g)
                if not first:
                    list_rows(g - 1)

            group(0, first=True)
            with pool.Fori(1, NG - 1) as g:
                group(g)
            group(NG - 1, last=True)
            power(rstd_a, avar_ready, apow_done, NG)
            power(rstd_h, hvar_ready, hpow_done, NG)
            list_rows(NG - 1)

            def send(i, j):
                pool.wait_ge(y_ready[j % 2], i * 2 + j // 2 + 1)
                pool.sem_inc(waited, 1)
                pool.indirect_dma_start(
                    out=out.rearrange("b p d -> (b p) d"),
                    out_offset=bass.IndirectOffsetOnAxis(ap=xs_sb[j][:, TOKEN:TOKEN + 1].bitcast(I32), axis=0),
                    in_=y_sb[j], in_offset=None, bounds_check=B * P - 1, oob_is_err=False).then_inc(sent[j], 16)

            with pool.Fori(0, NS // NB) as i:
                for j in range(NB):
                    send(i, j)
            for j in range(NS % NB):
                send(NS // NB, j)

        @block.tensor
        def _(pe):
            first_banks = [ps_s[:, 0:512], ps_s[:, 512:1024], ps_acc[:, 0:512], ps_acc[:, 512:1024]]
            pe.wait_ge(pool_made, 4)
            pe.wait_ge(rows_in, 16 * N_ROWS)
            pe.transpose(ps_o[:, 0:P], as_rows[:, :], ident[:, :]).then_inc(cols_ps, 1)

            def turn_x(bank, k):
                for b in range(GT):
                    ins = pe.transpose(bank[:, b * P:(b + 1) * P], xn_cur[:, b, k * P:(k + 1) * P], ident[:, :])
                return ins

            for c in range(2):
                pe.wait_ge(c_in, 16)
                for b in range(GT):
                    ins = pe.transpose(first_banks[c][0:CC, b * P:(b + 1) * P],
                                       ctx_sb[:, b, c * CC:(c + 1) * CC], ident[:, :])
                ins.then_inc(turned, 1)
            for k in range(KD):
                pe.wait_ge(xn_ready, 1)
                turn_x(first_banks[2 + k], k).then_inc(turned, 1)

            def project(g, hp, first_unit=False):
                n = g * HP + hp
                tok = ds(g * GP, GP)
                if not first_unit:
                    pe.wait_ge(v_ready, n)
                if hp == 0 and not first_unit:
                    pe.wait_ge(ctxT_ready, 2 * g)
                for c in range(2):
                    ins = pe.matmul(ps_kv[:, :], wkv_sb[0:CC, c, hp * P:(hp + 1) * P], ctxT[0:CC, c, tok],
                                    start=(c == 0), stop=(c == 1))
                ins.then_inc(proj_k, 1)
                if not first_unit:
                    pe.wait_ge(q_ready, n)
                for k in range(KD):
                    ins = pe.matmul(ps_q[:, :], wq_sb[:, k, hp * P:(hp + 1) * P], xT[:, k, tok],
                                    start=(k == 0), stop=(k == KD - 1))
                ins.then_inc(proj_q, 1)
                pe.wait_ge(k_ready, 2 * n + 2)
                if hp == 0:
                    pe.wait_ge(ctx_cur_ready, g + 1)
                for b in range(GT):
                    for c in range(2):
                        ins = pe.matmul(ps_kv[:, b * P:(b + 1) * P], ctx_cur[0:CC, c, b * P:(b + 1) * P],
                                        wkv_sb[0:CC, c, INNER + hp * P:INNER + (hp + 1) * P],
                                        start=(c == 0), stop=(c == 1))
                ins.then_inc(proj_v, 1)

            def null_scores(xt, bank):
                for b in range(GT):
                    for k in range(KD):
                        ins = pe.matmul(bank[:, b * H:(b + 1) * H], xt[:, k, b * P:(b + 1) * P], wqn[:, k, :],
                                        start=(k == 0), stop=(k == KD - 1))
                return ins

            def add_out(g, hp):
                pe.wait_ge(oT_ready, g * HP + hp + 1)
                if hp == 0:
                    pe.wait_ge(acc_free, g)
                for b in range(GT):
                    ins = pe.matmul(ps_acc[:, b * D:(b + 1) * D], oT[:, b * P:(b + 1) * P], wout_sb[:, hp, :],
                                    start=(hp == 0 and b % 2 == 0), stop=False, skip_group_check=True)
                ins.then_inc(out_added, 1)

            def side(g, hp, first, last):
                if (first and hp in (4, 5, 7)) or (last and hp < 4):
                    return
                if not (first and hp == 0):
                    pe.wait_ge(side_free, task(g, hp))
                if hp < 2:
                    pe.wait_ge(c_in, 16 * (g + 2))
                    for b in range(GT):
                        ins = pe.transpose(ps_side[0:CC, b * P:(b + 1) * P],
                                           ctx_sb[:, b, hp * CC:(hp + 1) * CC], ident[:, :])
                elif hp < 4:
                    pe.wait_ge(xn_ready, g + 2)
                    ins = turn_x(ps_side, hp - 2)
                elif hp < 6:
                    pe.wait_ge(h2_ready, g)
                    for b in range(GT):
                        ins = pe.transpose(ps_side[:, b * P:(b + 1) * P],
                                           stage[:, b, D + (hp - 4) * P:D + (hp - 3) * P], ident[:, :])
                elif hp == 6:
                    if not first:
                        for b in range(GT):
                            for k in range(KD):
                                ins = pe.matmul(ps_side[:, b * E:(b + 1) * E], h2T[:, k, b * P:(b + 1) * P],
                                                wr_sb[:, k, :], start=(k == 0), stop=(k == KD - 1))
                    if not last:
                        pe.wait_ge(xT_cur_ready, g + 1)
                        ins = null_scores(xT_cur, ps_side[:, P:2 * P])
                else:
                    pe.wait_ge(onehot_ready, g)
                    pe.matmul(ps_side[:, 0:GT * E], before[:, :], onehot[:, :, :], start=True, stop=True)
                    ins = pe.matmul(ps_side[:, P:P + GT * E], ones_bf[:, :],
                                    onehot[:, :, :].rearrange("p t e -> p e t"), start=True, stop=True)
                ins.then_inc(side_ps, 1)

            def group(g, first=False, last=False):
                for hp in range(HP):
                    n = g * HP + hp
                    pe.wait_ge(q_ready, n + 1)
                    pe.wait_ge(k_ready, 2 * n + 2)
                    for half in range(2):
                        if not (first and hp == 0):
                            pe.wait_ge(pT_hi if half else pT_lo, n)
                        bias = mask_bias[:, ds(g * GT + 2 * half, 2), :].unsqueeze(2).broadcast_to([P, 2, 2, P])
                        pe.matmul(ps_s[:, half * 512:(half + 1) * 512], row0_one[:, :], bias,
                                  start=True, stop=False, skip_group_check=True)
                        for b in (2 * half, 2 * half + 1):
                            ins = pe.matmul(ps_s[:, b * 2 * P:(b + 1) * 2 * P], qT[:, b * P:(b + 1) * P],
                                            kT[:, b, :], start=False, stop=True, skip_group_check=True)
                        ins.then_inc(scored, 1)
                    if hp + 1 < HP:
                        project(g, hp + 1)
                    elif not last:
                        project(g + 1, 0)
                    side(g, hp, first, last)
                    for half in range(2):
                        pe.wait_ge(probs_ready, 2 * n + half + 1)
                        for j in range(GT * half, GT * half + GT):
                            ins = pe.transpose(ps_s[:, j * P:(j + 1) * P], probs[:, j, :], ident[:, :])
                        ins.then_inc(probs_turned, 1)
                    if hp > 0:
                        add_out(g, hp - 1)
                    pe.wait_ge(v_ready, n + 1)
                    if hp == 0 and not first:
                        pe.wait_ge(null_pT_ready, g)
                    if not (first and hp == 0):
                        pe.wait_ge(oT_ready, n)
                    for b in range(GT):
                        if b == 0:
                            pe.wait_ge(pT_lo, n + 1)
                        if b == GT // 2:
                            pe.wait_ge(pT_hi, n + 1)
                        for h in range(2):
                            ins = pe.matmul(ps_o[h * DH:(h + 1) * DH, b * P:(b + 1) * P],
                                            v_sb[hp % 2][:, b, h * DH:(h + 1) * DH], probsT[:, 2 * b + h, :],
                                            start=True, stop=True, skip_group_check=True)
                    ins.then_inc(weighed, 1)
                pe.wait_ge(oT_ready, g * HP + HP)
                pe.wait_ge(null_p_ready, 2 * HP * (g + 1))
                pe.transpose(ps_o[:, 0:P], null_p[:, :], ident[:, :]).then_inc(null_turned, 1)
                add_out(g, HP - 1)
                pe.wait_ge(null_pT_ready, g + 1)
                for b in range(GT):
                    ins = pe.matmul(ps_acc[:, b * D:(b + 1) * D], null_pT[:, :], nw_rows[:, b, :],
                                    start=False, stop=True, skip_group_check=True)
                ins.then_inc(acc_done, 1)

            pe.wait_ge(pool_made, 9)
            pe.wait_ge(wkv_in, 16)
            pe.wait_ge(copied, 4)
            pe.wait_ge(wq_in, 16)
            project(0, 0, first_unit=True)
            pe.wait_ge(wqn_ready, 1)
            null_scores(xT, ps_o).then_inc(null_ps, 1)
            pe.wait_ge(mask_ready, 1)
            pe.wait_ge(nsn_ready, 1)
            pe.wait_ge(nvd_ready, 1)
            pe.wait_ge(wout_in, 16)
            for c in range(HP):
                ins = pe.matmul(ps_o[:, 0:D], nv_diag[:, c, :], wout_sb[:, c, :],
                                start=(c == 0), stop=(c == HP - 1))
            ins.then_inc(nw_ps, 1)
            pe.wait_ge(nw_ready, 1)
            group(0, first=True)
            with pe.Fori(1, NG - 1) as g:
                group(g)
            group(NG - 1, last=True)
            for hp in range(4, HP):
                side(NG, hp, False, True)
            pe.wait_ge(tables_ready, 1)

            ps_h = [ps_s, ps_acc]
            ps_y = [ps_q, ps_kv]
            ps_x = [ps_side, ps_o]

            def turn_rows(i, j, k):
                par = j % 2
                pe.wait_ge(xs_in[j], 16 * (i + 1))
                if not (isinstance(k, int) and k == 0):
                    pe.wait_ge(xsT_ready[par], k)
                for c in range(KD):
                    ins = pe.transpose(ps_x[par][:, c * P:(c + 1) * P],
                                       xs_sb[j][:, D + c * P:D + (c + 1) * P], ident[:, :])
                ins.then_inc(xs_turned[par], 1)

            def tile(i, j, last=False):
                par, k = j % 2, i * 2 + j // 2
                pe.wait_ge(w1_in[j], 16 * (i + 1))
                pe.wait_ge(xsT_ready[par], k + 1)
                pe.wait_ge(h_sb[par], FC * k)
                for f in range(FC):
                    for c in range(KD):
                        ins = pe.matmul(ps_h[par][:, f * P:(f + 1) * P], w1_sb[j][:, c, f * P:(f + 1) * P],
                                        xsT[par][:, c, :], start=(c == 0), stop=(c == KD - 1))
                    if f % 4 == 3:
                        ins.then_inc(h_ps[par], 1)
                if not last and j + 1 < NB:
                    turn_rows(i, j + 1, i * 2 + (j + 1) // 2)
                elif not last:
                    turn_rows(i + 1, 0, i * 2 + 2)
                pe.wait_ge(w2_in[j], 16 * (i + 1))
                pe.wait_ge(y_ready[par], k)
                for f in range(FC):
                    pe.wait_ge(h_sb[par], FC * k + f + 1)
                    ins = pe.matmul(ps_y[par][:, 0:D], hT[par][:, f, :], w2_sb[j][:, f, :],
                                    start=(f == 0), stop=(f == FC - 1))
                ins.then_inc(y_ps[par], 1)

            turn_rows(0, 0, 0)
            for j in range(NB):
                tile(0, j)
            with pe.Fori(1, NS // NB) as i:
                for j in range(NB):
                    tile(i, j)
            for j in range(NS % NB):
                tile(NS // NB, j, last=(j == NS % NB - 1))

        @block.scalar
        def _(act):
            act.wait_ge(pool_made, 1)
            act.dma_start(as_rows[0:E * FC, :], b_1.rearrange("e (c p) -> (e c) p", p=P)).then_inc(rows_in, 16)
            act.dma_start(as_rows[E * FC:E * FC + KD, :], g_norm.rearrange("(k p) -> k p", p=P)).then_inc(rows_in, 16)
            for half in range(2):
                act.dma_start(as_rows[E * FC + KD:E * FC + KD + 1, half * DH:(half + 1) * DH],
                              null_kv[1:2, :]).then_inc(rows_in, 16)
            act.dma_start(nk_row[:, :], null_kv[0:1, :].broadcast_to([P, DH])).then_inc(small_in, 16)
            act.dma_start(mask_u8[:, :], mask.rearrange("b n -> (b n)").rearrange("(a n) -> a n", a=1)
                          ).then_inc(small_in, 16)
            act.dma_start(gates[:, 0:1], row_of(g_xattn)).then_inc(small_in, 16)
            act.dma_start(gates[:, 1:2], row_of(g_ffn)).then_inc(small_in, 16)
            act.dma_start(gout_row[:, :], row_of(g_out)).then_inc(small_in, 16)
            act.dma_start(wr_sb[:, :, :], w_r.rearrange("(k p) e -> p k e", p=P)).then_inc(small_in, 16)
            act.wait_ge(cols_ps, 1)
            act.activation(as_cols[:, :], ps_o[:, 0:P], ACT.Copy).then_inc(cols_ready, 1)
            act.wait_ge(cols_ready, 1)
            first_banks = [ps_s[:, 0:512], ps_s[:, 512:1024], ps_acc[:, 0:512], ps_acc[:, 512:1024]]
            for c in range(2):
                act.wait_ge(turned, c + 1)
                act.activation(ctxT[0:CC, c, 0:GP], first_banks[c][0:CC], ACT.Copy).then_inc(copied, 1)
            for k in range(KD):
                act.wait_ge(turned, 3 + k)
                act.activation(xT[:, k, 0:GP], first_banks[2 + k], ACT.Copy, scale=gn_col[:, k:k + 1]
                               ).then_inc(copied, 1)

            def take_q(n, first_unit=False):
                act.wait_ge(proj_q, n + 1)
                if not first_unit:
                    act.wait_ge(scored, 2 * n)
                act.activation(qT, ps_q[:, :], ACT.Copy).then_inc(q_ready, 1)

            def side(g, hp, first, last):
                if hp < 4 and not last:
                    act.wait_ge(side_ps, task(g, hp) + 1)
                    tok = ds((g + 1) * GP, GP)
                    if hp < 2:
                        act.activation(ctxT[0:CC, hp, tok], ps_side[0:CC], ACT.Copy).then_inc(ctxT_ready, 1)
                        act.wait_ge(ctxT_ready, 2 * g + hp + 1)
                        act.sem_inc(side_free, 1)
                    else:
                        act.activation(xT[:, hp - 2, tok], ps_side[:, :], ACT.Copy,
                                       scale=gn_col[:, hp - 2:hp - 1]).then_inc(side_free, 1)
                elif hp in (4, 5) and not first:
                    act.wait_ge(side_ps, task(g, hp) + 1)
                    act.activation(h2T[:, hp - 4, :], ps_side[:, :], ACT.Copy).then_inc(side_free, 1)
                elif hp == 6 and not first:
                    act.wait_ge(df_ready, g)
                    act.activation(r_b[:, :, :], r_a[:, :, :], ACT.Exp).then_inc(ex_ready, 1)

            def group(g, first=False, last=False):
                for hp in range(HP):
                    n = g * HP + hp
                    for half in range(2):
                        m, b2 = 2 * n + half, slice(2 * half, 2 * half + 2)
                        act.wait_ge(diff_ready, m + 1)
                        act.activation(null_exp[:, b2, :], null_diff[:, b2, :], ACT.Exp).then_inc(null_exp_done, 1)
                        act.wait_ge(nmax_ready, m + 1)
                        if not (first and hp == 0):
                            act.wait_ge(probs_turned, m - 1)
                        for j in range(GT * half, GT * half + GT):
                            ins = act.activation(probs[:, j, :], ps_s[:, j * P:(j + 1) * P], ACT.Exp,
                                                 bias=nmax[:, j // 2, j % 2:j % 2 + 1], scale=SCALE,
                                                 accum_out=sums[:, j // 2, j % 2:j % 2 + 1])
                        ins.then_inc(exp_done, 1)
                    if hp + 1 < HP or not last:
                        take_q(n + 1)
                    if hp != 6:
                        side(g, hp, first, last)
                    act.wait_ge(probs_turned, 2 * n + 1)
                    if not (first and hp == 0):
                        act.wait_ge(weighed, n)
                    act.activation(probsT[:, 0:GT, :], ps_s[:, 0:512].rearrange("p (j n) -> p j n", j=GT),
                                   ACT.Copy).then_inc(pT_lo, 1)
                    act.wait_ge(weighed, n + 1)
                    if not (first and hp == 0):
                        act.wait_ge(out_added, n)
                    act.activation(oT, ps_o[:, :], ACT.Copy).then_inc(oT_ready, 1)
                    if hp == 6:
                        side(g, hp, first, last)
                act.wait_ge(null_turned, g + 1)
                act.activation(null_pT[:, :], ps_o[:, 0:P], ACT.Copy).then_inc(null_pT_ready, 1)

            take_q(0, first_unit=True)
            act.wait_ge(small_in, 16 * N_SMALL)
            act.activation(tanhs[:, :], gates[:, :], ACT.Tanh).then_inc(act_setup, 1)
            group(0, first=True)
            with act.Fori(1, NG - 1) as g:
                group(g)
            group(NG - 1, last=True)
            for hp in range(4, HP):
                side(NG, hp, False, True)

            ps_h = [ps_s, ps_acc]

            def tile(i, j):
                par, k = j % 2, i * 2 + j // 2
                act.wait_ge(b1_ready[par], k + 1)
                act.wait_ge(y_ps[par], k)
                for f in range(FC):
                    if f % 4 == 0:
                        act.wait_ge(h_ps[par], 2 * k + f // 4 + 1)
                    act.activation(hT[par][:, f, :], ps_h[par][:, f * P:(f + 1) * P], ACT.Gelu,
                                   bias=b1_cur[par][:, f:f + 1]).then_inc(h_sb[par], 1)

            for j in range(NB):
                tile(0, j)
            with act.Fori(1, NS // NB) as i:
                for j in range(NB):
                    tile(i, j)
            for j in range(NS % NB):
                tile(NS // NB, j)

        @block.vector
        def _(dve):
            chained = [0]

            def link(ins):
                chained[0] += 1
                ins.then_inc(dve_chain, 1)
                dve.wait_ge(dve_chain, chained[0])

            def statistics(src, step, mv, rstd, scale, shift, ready):
                for b in range(GT):
                    ins = dve.bn_stats(stats[:, b, :], src(b))
                step(ins)
                dve.sem_inc(waited, 1)
                for b in range(GT):
                    ins = dve.bn_aggr(mv[:, b, :], stats[:, b, :])
                step(ins)
                dve.tensor_scalar(rstd[:, :], mv[:, :, 1], scale, shift, ALU.mult, ALU.add).then_inc(ready, 1)

            def x_rows(g, b):
                return x_sb[:, ds(g * GT + b, 1), :].rearrange("p a d -> p (a d)")

            def stats_x(g):
                count = [0]

                def step(ins):
                    count[0] += 1
                    ins.then_inc(x_step, 1)
                    dve.wait_ge(x_step, g * X_STEPS + count[0])

                statistics(lambda b: x_rows(g, b), step, mv_x, rstd_x, 1.0 + EPS, EPS * EPS, xvar_ready)
                assert count[0] == X_STEPS

            def norm_x(g):
                dve.wait_ge(xpow_done, g + 1)
                for b in range(GT):
                    ins = dve.tensor_scalar(xn_cur[:, b, :], x_rows(g, b), mv_x[:, b, 0:1], rstd_x[:, b:b + 1],
                                            ALU.subtract, ALU.mult)
                ins.then_inc(xn_ready, 1)

            dve.wait_ge(x_in[0], 16)
            stats_x(0)
            norm_x(0)
            dve.wait_ge(small_in, 16 * N_SMALL)
            dve.wait_ge(pool_made, 8)
            dve.tensor_scalar(mask_bias[0:1, :, :].rearrange("p b n -> p (b n)"), mask_u8[:, :], -1.0, MASKED,
                              ALU.add, ALU.mult).then_inc(mask_ready, 1)
            dve.wait_ge(wq_in, 16)
            link(dve.tensor_tensor(nk_prod[:, :, :], wq_sb.rearrange("p k (h d) -> p (k h) d", h=H),
                                   over(nk_row[:, :], 1, KD * H), ALU.mult))
            dve.tensor_reduce(wqn[:, :, :].rearrange("p k h -> p (k h)"), nk_prod[:, :, :], AX_X, ALU.add
                              ).then_inc(wqn_ready, 1)

            def take_k(n, first_unit=False):
                dve.wait_ge(proj_k, n + 1)
                if not first_unit:
                    dve.wait_ge(scored, 2 * n)
                for h in range(2):
                    p = slice(h * DH, (h + 1) * DH)
                    dve.tensor_copy(kT[p, :, h * P:(h + 1) * P], ps_kv[p, :].rearrange("p (b n) -> p b n", b=GT)
                                    ).then_inc(k_ready, 1)

            def take_v(n, par, early=False):
                dve.wait_ge(proj_v, n + 1)
                if not early:
                    dve.wait_ge(weighed, n - 1)
                dve.tensor_copy(v_sb[par], ps_kv[:, :].rearrange("p (b n) -> p b n", b=GT)).then_inc(v_ready, 1)

            def take_null_scores(g, bank):
                ins = dve.tensor_scalar(nsn[:, ds(g * GT, GT), :].rearrange("p b h -> p (b h)"), bank, -SCALE,
                                        None, ALU.mult)
                ins.then_inc(nsn_ready, 1)

            take_k(0, first_unit=True)
            take_v(0, 0, early=True)
            dve.wait_ge(cols_ready, 1)
            dve.wait_ge(pool_made, 15)
            dve.tensor_scalar(nv_diag[:, :, :], nv_diag[:, :, :], nv_col[:, 0:1], None, ALU.mult).then_inc(nvd_ready, 1)
            dve.wait_ge(null_ps, 1)
            take_null_scores(0, ps_o[:, 0:GT * H])
            dve.wait_ge(act_setup, 1)
            link(dve.tensor_scalar(gout_row[:, :], gout_row[:, :], tanhs[:, 0:1], None, ALU.mult))
            dve.wait_ge(pool_made, 27)
            link(dve.tensor_copy(iota_s[:, :], iota_i[:, :]))
            link(dve.tensor_scalar(iota_e8[:, :], iota_s[:, 0:E], float(-E), None, ALU.add))
            link(dve.tensor_scalar(region[:, :], iota_s[:, 0:E], float(CAP), None, ALU.mult))
            dve.wait_ge(nw_ps, 1)
            for b in range(GT):
                ins = dve.tensor_scalar(nw_rows[:, b, :], ps_o[:, 0:D], rows_of[:, b:b + 1], None, ALU.mult)
            ins.then_inc(nw_ready, 1)

            count = [0]

            def router(last, part):
                def step(ins):
                    count[0] += 1
                    ins.then_inc(f_step, 1)
                    dve.wait_ge(f_step, last * F_STEPS + count[0])

                x2 = stage[:, :, 0:D]
                h2 = stage[:, :, D:2 * D]
                if part == 0:
                    count[0] = 0
                    statistics(lambda b: att_cur[:, b, :], step, mv_a, rstd_a, 1.0, EPS, avar_ready)
                elif part == 1:
                    for b in range(GT):
                        ins = dve.scalar_tensor_tensor(out=att_cur[:, b, :], in0=att_cur[:, b, :],
                                                       scalar=mv_a[:, b, 0:1], in1=gout_row[:, :],
                                                       op0=ALU.subtract, op1=ALU.mult)
                    step(ins)
                    dve.wait_ge(apow_done, last + 1)
                    dve.wait_ge(stage_free, last + 1)
                    for b in range(GT):
                        ins = dve.scalar_tensor_tensor(out=x2[:, b, :], in0=att_cur[:, b, :],
                                                       scalar=rstd_a[:, b:b + 1], in1=x_rows(last, b),
                                                       op0=ALU.mult, op1=ALU.add)
                    step(ins)
                elif part == 2:
                    statistics(lambda b: x2[:, b, :], step, mv_h, rstd_h, 1.0, EPS, hvar_ready)
                elif part == 3:
                    dve.wait_ge(hpow_done, last + 1)
                    for b in range(GT):
                        ins = dve.tensor_scalar(h2[:, b, :], x2[:, b, :], mv_h[:, b, 0:1], rstd_h[:, b:b + 1],
                                                ALU.subtract, ALU.mult)
                    ins.then_inc(h2_ready, 1)
                    step(dve.tensor_copy(stage[:, :, TOKEN:TOKEN + 1].bitcast(I32).rearrange("p b a -> p (b a)"),
                                         token_i[:, ds(last * GT, GT)]))
                elif part == 6:
                    flat = "p t e -> p (t e)"
                    step(dve.tensor_copy(logits[:, :, :].rearrange(flat), ps_side[:, 0:GT * E]))
                    step(dve.tensor_reduce(r_max[:, :], logits[:, :, :], AX_X, ALU.max))
                    largest = over(r_max[:, :], 2, E)
                    dve.tensor_tensor(r_a[:, :, :], logits[:, :, :], largest, ALU.subtract).then_inc(df_ready, 1)
                    step(dve.tensor_tensor(logits[:, :, :], logits[:, :, :], largest, ALU.is_equal))
                    step(dve.tensor_tensor(logits[:, :, :], logits[:, :, :], over(iota_e8[:, :], 1, GT), ALU.mult))
                    step(dve.tensor_reduce(first_e[:, :], logits[:, :, :], AX_X, ALU.min))
                    dve.tensor_tensor(onehot[:, :, :], over(iota_e8[:, :], 1, GT), over(first_e[:, :], 2, E),
                                      ALU.is_equal).then_inc(onehot_ready, 1)
                elif part == 7:
                    dve.wait_ge(ex_ready, last + 1)
                    step(dve.tensor_reduce(r_sum[:, :], r_b[:, :, :], AX_X, ALU.add))
                    step(dve.reciprocal(r_max[:, :], r_sum[:, :]))
                    step(dve.tensor_scalar(stage[:, :, COEF:COEF + 1].rearrange("p b a -> p (b a)"), r_max[:, :],
                                           tanhs[:, 1:2], None, ALU.mult))
                    flat = "p e t -> p (e t)"
                    dve.wait_ge(side_ps, task(last + 1, 7) + 1)
                    step(dve.tensor_copy(counts[:, :, :].rearrange(flat), ps_side[:, P:P + GT * E]))
                    step(dve.tensor_tensor_scan(upto[:, :, :].rearrange(flat), keep_scan[:, :, :].rearrange(flat),
                                                counts[:, :, :].rearrange(flat), 0.0, ALU.mult, ALU.add))
                    step(dve.tensor_tensor(base[:, :, :], upto[:, :, :], counts[:, :, :], ALU.subtract))
                    step(dve.tensor_tensor(base[:, :, :], base[:, :, :], over(taken[:, :], 2, GT), ALU.add))
                    step(dve.tensor_tensor(base[:, :, :], base[:, :, :], over(region[:, :], 2, GT), ALU.add))
                    step(dve.tensor_tensor(r_a[:, :, :], ps_side[:, 0:GT * E].rearrange("p (t e) -> p t e", e=E),
                                           base[:, :, :].rearrange("p e t -> p t e"), ALU.add))
                    dve.sem_inc(side_free, 1)
                    step(dve.tensor_tensor(r_a[:, :, :], r_a[:, :, :], onehot[:, :, :], ALU.mult))
                    step(dve.tensor_reduce(pos_f[:, :], r_a[:, :, :], AX_X, ALU.add))
                    step(dve.tensor_copy(pos_i[:, :], pos_f[:, :]))
                    step(dve.tensor_tensor(taken[:, :], taken[:, :], upto[:, :, GT - 1], ALU.add))
                    dve.sem_inc(placed, 1)
                    assert count[0] == F_STEPS, count[0]

            def beside(g, hp, first, last):
                if hp == 0 and not first:
                    router(g - 1, 0)
                if hp == 0 and not last:
                    if first:
                        for later in range(1, NG):
                            dve.wait_ge(x_in[later], 16)
                    stats_x(g + 1)
                if hp == 1 and not last:
                    norm_x(g + 1)
                if hp in (1, 2, 3) and not first:
                    router(g - 1, hp)
                if hp == 6:
                    dve.wait_ge(side_ps, task(g, 6) + 1)
                    if not last:
                        take_null_scores(g + 1, ps_side[:, P:P + GT * H])
                        dve.wait_ge(nsn_ready, g + 2)
                    if not first:
                        router(g - 1, 6)
                    dve.sem_inc(side_free, 1)
                if hp == 7 and not first:
                    router(g - 1, 7)

            def group(g, first=False, last=False):
                for hp in range(HP):
                    n = g * HP + hp
                    pair = slice(2 * hp, 2 * hp + 2)
                    for half in range(2):
                        m, b2 = 2 * n + half, slice(2 * half, 2 * half + 2)
                        null = nsn[:, ds(g * GT + 2 * half, 2), pair]
                        dve.wait_ge(scored, m + 1)
                        dve.tensor_reduce(rowmax[:, b2, :].rearrange("p b h -> p (b h)"),
                                          ps_s[:, half * 512:(half + 1) * 512].rearrange("p (j n) -> p j n", n=P),
                                          AX_X, ALU.max).then_inc(row_max, 1)
                        dve.wait_ge(row_max, m + 1)
                        if not (first and hp == 0):
                            dve.wait_ge(exp_done, m - 1)
                        dve.scalar_tensor_tensor(out=nmax[:, b2, :], in0=rowmax[:, b2, :], scalar=-SCALE, in1=null,
                                                 op0=ALU.mult, op1=ALU.min).then_inc(nmax_ready, 1)
                        dve.wait_ge(nmax_ready, m + 1)
                        dve.tensor_tensor(null_diff[:, b2, :], nmax[:, b2, :], null, ALU.subtract
                                          ).then_inc(diff_ready, 1)
                    if hp + 1 < HP or not last:
                        take_k(n + 1)
                    for half in range(2):
                        m, b2 = 2 * n + half, slice(2 * half, 2 * half + 2)
                        dve.wait_ge(null_exp_done, m + 1)
                        dve.wait_ge(exp_done, m + 1)
                        dve.tensor_tensor(denom[:, b2, :], sums[:, b2, :], null_exp[:, b2, :], ALU.add
                                          ).then_inc(denom_ready, 1)
                        dve.wait_ge(denom_ready, m + 1)
                        dve.reciprocal(recip[:, b2, :], denom[:, b2, :]).then_inc(recip_ready, 1)
                        dve.wait_ge(recip_ready, m + 1)
                        part = probs[:, half * GT:(half + 1) * GT, :]
                        by = recip[:, b2, :].rearrange("p b h -> p (b h)")
                        dve.tensor_tensor(part, part, over(by, 2, P), ALU.mult).then_inc(probs_ready, 1)
                        if hp == 0 and not first:
                            dve.wait_ge(null_turned, g)
                        dve.tensor_tensor(null_p[:, 0:GT * H].rearrange("p (b h) -> p b h", h=H)[:, b2, pair],
                                          null_exp[:, b2, :], recip[:, b2, :], ALU.mult).then_inc(null_p_ready, 1)
                    if hp + 1 < HP or not last:
                        take_v(n + 1, (hp + 1) % 2, early=(first and hp == 0))
                    dve.wait_ge(probs_turned, 2 * n + 2)
                    if not (first and hp == 0):
                        dve.wait_ge(weighed, n)
                    dve.tensor_copy(probsT[:, GT:2 * GT, :], ps_s[:, 512:1024].rearrange("p (j n) -> p j n", j=GT)
                                    ).then_inc(pT_hi, 1)
                    beside(g, hp, first, last)
                dve.wait_ge(acc_done, g + 1)
                dve.tensor_copy(att_cur[:, :, :], ps_acc[:, :].rearrange("p (b n) -> p b n", b=GT)
                                ).then_inc(acc_free, 1)
                dve.wait_ge(acc_free, g + 1)

            group(0, first=True)
            with dve.Fori(1, NG - 1) as g:
                group(g)
            group(NG - 1, last=True)
            for part in (0, 1, 2, 3, 6, 7):
                if part == 6:
                    dve.wait_ge(side_ps, task(NG, 6) + 1)
                router(NG - 1, part)
                if part == 6:
                    dve.sem_inc(side_free, 1)

            link(dve.tensor_scalar(tiles_i[:, :], taken[:, :], float(P - 1), None, ALU.add))
            link(dve.tensor_tensor(fill_f[:, :], region[:, :], taken[:, :], ALU.add))
            link(dve.tensor_copy(fill_i[:, :], fill_f[:, :]))
            link(dve.tensor_scalar(tiles_i[:, :], tiles_i[:, :], P.bit_length() - 1, None, ALU.logical_shift_right))
            link(dve.tensor_copy(tiles_n[:, :], tiles_i[:, :]))
            link(dve.tensor_tensor_scan(ends[:, :], ones_e[:, :], tiles_n[:, :], 0.0, ALU.mult, ALU.add))
            link(dve.tensor_tensor(starts[:, :], ends[:, :], tiles_n[:, :], ALU.subtract))
            by_tile = over(iota_s[:, :], 2, E)
            link(dve.tensor_tensor(has[:, :, :], over(ends[:, :], 1, NS), by_tile, ALU.is_gt))
            link(dve.tensor_tensor(t_a[:, :, :], over(starts[:, :], 1, NS), by_tile, ALU.is_gt))
            link(dve.tensor_tensor(has[:, :, :], has[:, :, :], t_a[:, :, :], ALU.subtract))
            link(dve.tensor_tensor(t_a[:, :, :], has[:, :, :], over(iota_s[:, 0:E], 1, NS), ALU.mult))
            link(dve.tensor_reduce(tile_f[:, :], t_a[:, :, :], AX_X, ALU.add))
            link(dve.tensor_copy(eid_i[:, :], tile_f[:, :]))
            link(dve.scalar_tensor_tensor(out=starts[:, :], in0=starts[:, :], scalar=float(-P), in1=region[:, :],
                                          op0=ALU.mult, op1=ALU.add))
            link(dve.tensor_tensor(t_a[:, :, :], has[:, :, :], over(starts[:, :], 1, NS), ALU.mult))
            link(dve.tensor_reduce(tile_f[:, :], t_a[:, :, :], AX_X, ALU.add))
            link(dve.tensor_reduce(in_use[:, :], has[:, :, :], AX_X, ALU.add))
            link(dve.tensor_scalar(tile_g[:, :], iota_s[:, :], float(P), float(-FILL), ALU.mult, ALU.add))
            link(dve.tensor_tensor(tile_g[:, :], tile_g[:, :], in_use[:, :], ALU.mult))
            link(dve.scalar_tensor_tensor(out=tile_f[:, :], in0=tile_f[:, :], scalar=float(FILL), in1=tile_g[:, :],
                                          op0=ALU.add, op1=ALU.add))
            dve.tensor_copy(row_i[:, :], tile_f[:, :]).then_inc(tables_ready, 1)
            dve.wait_ge(tables_ready, 1)

            ps_y = [ps_q, ps_kv]
            ps_x = [ps_side, ps_o]

            def take_rows(par, k):
                dve.wait_ge(xs_turned[par], k + 1)
                if not (isinstance(k, int) and k == 0):
                    dve.wait_ge(h_ps[par], 2 * k)
                dve.tensor_copy(xsT[par], ps_x[par][:, 0:KD * P].rearrange("p (k n) -> p k n", k=KD)
                                ).then_inc(xsT_ready[par], 1)

            def tile(i, j, last=False):
                par, k = j % 2, i * 2 + j // 2
                e = dve.value_load(eid_i[0:1, ds(i * NB + j, 1)], min_val=0, max_val=E - 1)
                dve.wait_ge(h_sb[par], FC * k)
                dve.tensor_copy(b1_cur[par], b1T[:, ds(e * FC, FC)]).then_inc(b1_ready[par], 1)
                if not last:
                    take_rows((j + 1) % 2, i * 2 + (j + 1) // 2)
                dve.wait_ge(y_ps[par], k + 1)
                dve.wait_ge(b2_in[j], 16 * (i + 1))
                dve.wait_ge(sent[j], 16 * i)
                dve.tensor_tensor(y_sb[j], ps_y[par][:, 0:D], b2_sb[j], ALU.add).then_inc(y_added, 1)
                dve.wait_ge(y_added, i * NB + j + 1)
                dve.wait_ge(xs_in[j], 16 * (i + 1))
                dve.scalar_tensor_tensor(out=y_sb[j], in0=y_sb[j], scalar=xs_sb[j][:, COEF:COEF + 1],
                                         in1=xs_sb[j][:, 0:D], op0=ALU.mult, op1=ALU.add).then_inc(y_ready[par], 1)

            take_rows(0, 0)
            for j in range(NB):
                tile(0, j)
            with dve.Fori(1, NS // NB) as i:
                for j in range(NB):
                    tile(i, j)
            for j in range(NS % NB):
                tile(NS // NB, j, last=(j == NS % NB - 1))


_INS = ['x', 'ctx_768', 'mask_BxS2_bf1', 'g_xattn', 'g_ffn', 'L0_xattn_g_norm', 'L0_xattn_null_kv',
        'L0_xattn_Wq', 'L0_xattn_Wkv', 'L0_xattn_Wout', 'L0_xattn_g_out', 'L0_ffn_Wr', 'L0_ffn_W1',
        'L0_ffn_b1', 'L0_ffn_W2', 'L0_ffn_b2']
_OUTS = [((16, 128, 256), 'float32')]


def kernel(**inputs):
    import numpy as _np
    import concourse.bacc as _bacc
    from concourse import mybir as _mybir
    from concourse.bass_utils import run_bass_kernel_spmd as _run

    nc = _bacc.Bacc("TRN2", target_bir_lowering=False, num_devices=1)
    arrays, args = {}, []
    for name in _INS:
        a = _np.ascontiguousarray(inputs[name])
        if a.dtype.kind == "b":
            a = a.view(_np.uint8)
        arrays[f"in_{name}_dram"] = a
        args.append(nc.dram_tensor(f"in_{name}_dram", a.shape, _mybir.dt.from_np(a.dtype), kind="ExternalInput").ap())
    for i, (shape, dtype) in enumerate(_OUTS):
        dt = _mybir.dt.from_np(_np.dtype(dtype))
        args.append(nc.dram_tensor(f"out_{i}_dram", shape, dt, kind="ExternalOutput").ap())
    flamingo_layer(nc, *args)
    r = _run(nc, [arrays], core_ids=[0])
    got = tuple(r.results[0][f"out_{i}_dram"] for i in range(len(_OUTS)))
    return got[0]
```

```python
from contextlib import ExitStack

import concourse.bass as bass
from concourse import mybir

P = 128
ALU = mybir.AluOpType
ACT = mybir.ActivationFunctionType
F32 = mybir.dt.float32
F32R = mybir.dt.float32r
BF16 = mybir.dt.bfloat16
I32 = mybir.dt.int32
U8 = mybir.dt.uint8
AX_X = mybir.AxisListType.X
EPS = 1e-5
MASKED = 1e30
ds = bass.ds


def flamingo_layer(nc, x, ctx_in, mask, g_xattn, g_ffn, g_norm, null_kv, w_q, w_kv, w_out,
                   g_out, w_r, w_1, b_1, w_2, b_2, out):
    B, N, D = x.shape
    C = ctx_in.shape[2]
    INNER = w_q.shape[1]
    DH = null_kv.shape[1]
    H = INNER // DH
    E, F = b_1.shape
    assert N == P and ctx_in.shape[1] == P and 2 * DH == P
    KD = D // P
    CC = C // 2
    HP = H // 2
    GT = 4
    GP = GT * P
    NG = B // GT
    SCALE = DH ** -0.5
    FC = F // P
    NS = B + E - 1
    EARLY = -(-((NG - 1) * GP - E * (P - 1)) // P)
    NL = NS - EARLY
    NU = B
    NB = 4
    assert EARLY == NB + 1 and NU % NB == 0
    CAP = B * P + P
    FILL = E * CAP
    ROW = D + 4
    COEF, TOKEN, MEAN, RSTD = D, D + 1, D + 2, D + 3
    NO_TOKEN = 2 * B * P

    with ExitStack() as ctx:
        def sb(name, shape, dt=F32):
            return ctx.enter_context(nc.sbuf_tensor(name, shape, dt))

        def sem(name):
            return ctx.enter_context(nc.semaphore(name))

        rows_list = nc.dram_tensor("rows_list", (FILL + P, ROW), F32).ap()

        x_sb = sb("x_sb", [P, B, D])
        xn_cur = sb("xn_cur", [P, GT, D])
        ctx_cur = sb("ctx_cur", [P, 2, GP])
        xT_next = sb("xT_next", [P, KD, GP])
        wout_sb = sb("wout_sb", [P, HP, D])
        ident = sb("ident", [P, P])
        row0_one = sb("row0_one", [P, P], BF16)
        mask_u8 = sb("mask_u8", [1, B * P], U8)
        mask_bias = sb("mask_bias", [P, B, P], BF16)
        before = sb("before", [P, P], BF16)
        ones_bf = sb("ones_bf", [P, P], BF16)
        gout_row = sb("gout_row", [P, D])
        nk_row = sb("nk_row", [P, DH])
        wr_sb = sb("wr_sb", [P, KD, E])
        gates = sb("gates", [P, 2])
        tanhs = sb("tanhs", [P, 2])
        stats = sb("stats", [P, GT, 6])
        mv_x = sb("mv_x", [P, B, 2])
        mv_a = sb("mv_a", [P, GT, 2])
        mv_h = sb("mv_h", [P, GT, 2])
        rstd_x = sb("rstd_x", [P, B])
        mean_cur = sb("mean_cur", [P, GT])
        rstd_cur = sb("rstd_cur", [P, GT])
        rstd_a = sb("rstd_a", [P, GT])
        rstd_h = sb("rstd_h", [P, GT])
        minus_half = sb("minus_half", [P, GT])
        wqn = sb("wqn", [P, KD, H])
        nv_diag = sb("nv_diag", [P, HP, P])
        rows_of = sb("rows_of", [P, GT])
        warm = sb("warm", [P, 1])
        nw_rows = sb("nw_rows", [P, GT, D])
        nsn = sb("nsn", [P, B, H])
        rowmax = sb("rowmax", [P, GT, 2])
        nmax = sb("nmax", [P, GT, 2])
        null_diff = sb("null_diff", [P, GT, 2])
        null_exp = sb("null_exp", [P, GT, 2])
        sums = sb("sums", [P, GT, 2])
        denom = sb("denom", [P, GT, 2])
        recip = sb("recip", [P, GT, 2])
        null_p = sb("null_p", [P, P])
        null_pT = sb("null_pT", [P, P])
        logits = sb("logits", [P, GT, E])
        onehot = sb("onehot", [P, GT, E], BF16)
        r_a = sb("r_a", [P, GT, E])
        r_b = sb("r_b", [P, GT, E])
        r_max = sb("r_max", [P, GT])
        r_sum = sb("r_sum", [P, GT])
        first_e = sb("first_e", [P, GT])
        token_i = sb("token_i", [P, B], I32)
        iota_i = sb("iota_i", [P, NS], I32)
        iota_s = sb("iota_s", [P, NS])
        iota_e8 = sb("iota_e8", [P, E])
        region = sb("region", [P, E])
        taken = sb("taken", [P, E])
        keep_scan = sb("keep_scan", [P, E, GT])
        counts = sb("counts", [P, E, GT])
        upto = sb("upto", [P, E, GT])
        base = sb("base", [P, E, GT])
        pos_f = sb("pos_f", [P, GT])
        pos_i = sb("pos_i", [P, GT], I32)
        done_early = sb("done_early", [P, E])
        tiles_i = sb("tiles_i", [P, E], I32)
        tiles_n = sb("tiles_n", [P, E])
        ones_e = sb("ones_e", [P, E])
        ends = sb("ends", [P, E])
        starts = sb("starts", [P, E])
        has = sb("has", [P, NS, E])
        t_a = sb("t_a", [P, NS, E])
        in_use = sb("in_use", [P, NS])
        tile_f = sb("tile_f", [P, NS])
        tile_g = sb("tile_g", [P, NS])
        eid_i = sb("eid_i", [P, NS], I32)
        row_i = sb("row_i", [P, NS], I32)
        used_i = sb("used_i", [P, 1], I32)
        fill_f = sb("fill_f", [P, E])
        fill_i = sb("fill_i", [P, E], I32)
        filling = sb("filling", [P, ROW])
        as_rows = sb("as_rows", [P, P])
        as_cols = sb("as_cols", [P, P])
        b1T = as_cols[:, 0:E * FC]
        gn_col = as_cols[:, E * FC:E * FC + KD]
        nv_col = as_cols[:, E * FC + KD:E * FC + KD + 1]
        b2_sb = [sb(f"b2_sb{j}", [P, D])[:, :] for j in range(NB)]
        xs_sb = [sb(f"xs_sb{j}", [P, ROW])[:, :] for j in range(NB)]
        xn_s = [sb(f"xn_s{j}", [P, D])[:, :] for j in range(2)]
        b1_cur = [sb(f"b1_cur{j}", [P, FC])[:, :] for j in range(2)]

        def on(stack, name, shape, dt=F32):
            return stack.enter_context(nc.sbuf_tensor(name, shape, dt))[tuple(slice(0, n) for n in shape)]

        with ExitStack() as setup:
            wk_sb = on(setup, "wk_sb", [P, 2, INNER])
            wq_sb = on(setup, "wq_sb", [P, KD, INNER])
            nk_prod = on(setup, "nk_prod", [P, KD * H, DH])
        att_cur = sb("att_cur", [P, GT, D])
        stage = sb("stage", [P, GT, ROW])
        h2 = sb("h2", [P, GT, D])
        h2T = sb("h2T", [P, KD, GP])
        probs = sb("probs", [P, 2 * GT, P])
        probsT = sb("probsT", [P, 2 * GT, P])

        with ExitStack() as attention:
            ctx_sb = on(attention, "ctx_sb", [P, GT, C])
            wq_split = on(attention, "wq_split", [P, 2, KD, INNER], F32R)
            wk_split = on(attention, "wk_split", [P, 2, 2, INNER], F32R)
            wv_sb = on(attention, "wv_sb", [P, 2, INNER])
            ctx_next = on(attention, "ctx_next", [P, 2, GP])
            x_split = on(attention, "x_split", [P, 2, 2, KD, GP], F32R)
            ctx_split = on(attention, "ctx_split", [P, 2, 2, 2, GP], F32R)
            qT = on(attention, "qT", [P, GP])
            kT = on(attention, "kT", [P, GT, 2 * P])
            v_sb = [on(attention, f"v_sb{j}", [P, GT, P]) for j in range(2)]
            oT = on(attention, "oT", [P, GP])
        free_first = GT * C + 2 * KD * INNER + 4 * INNER + 2 * INNER + 2 * GP + 4 * KD * GP + 8 * GP
        with ExitStack() as experts:
            w1_sb = [on(experts, f"w1_sb{j}", [P, KD, F]) for j in range(NB)]
            w2_sb = [on(experts, f"w2_sb{j}", [P, FC, D]) for j in range(NB)]
            hT = [on(experts, f"hT{j}", [P, FC, P]) for j in range(2)]
            xsT = [on(experts, f"xsT{j}", [P, KD, P]) for j in range(2)]
            y_sb = [on(experts, f"y_sb{j}", [P, D]) for j in range(NB)]
        assert NB * (KD * F + FC * D + D) + 2 * (FC * P + KD * P) <= free_first

        ps_qv = ctx.enter_context(nc.psum_tensor("ps_qv", [P, 512], F32))
        ps_k = ctx.enter_context(nc.psum_tensor("ps_k", [P, 512], F32))
        ps_side = ctx.enter_context(nc.psum_tensor("ps_side", [P, 512], F32))
        ps_s = ctx.enter_context(nc.psum_tensor("ps_s", [P, 1024], F32))
        ps_acc = ctx.enter_context(nc.psum_tensor("ps_acc", [P, 1024], F32))
        ps_o = ctx.enter_context(nc.psum_tensor("ps_o", [P, 512], F32))
        ps_h = [ps_s, ps_acc]
        ps_y = [ps_qv[:, 0:D], ps_k[:, 0:D]]
        ps_x = [ps_qv[:, D:2 * D], ps_k[:, D:2 * D]]

        x_in = [sem(f"x_in{g}") for g in range(NG)]
        c_in = sem("c_in")
        rows_in = sem("rows_in")
        small_in = sem("small_in")
        nk_in = sem("nk_in")
        wq_in = sem("wq_in")
        wk_in = sem("wk_in")
        wv_in = sem("wv_in")
        w_high = sem("w_high")
        w_low = sem("w_low")
        ctx_split_ready = sem("ctx_split_ready")
        x_split_ready = sem("x_split_ready")
        wout_in = sem("wout_in")
        filled = sem("filled")
        listed = sem("listed")
        w1_in = [sem(f"w1_in{j}") for j in range(NB)]
        w2_in = [sem(f"w2_in{j}") for j in range(NB)]
        b2_in = [sem(f"b2_in{j}") for j in range(NB)]
        xs_in = [sem(f"xs_in{j}") for j in range(NB)]
        sent = [sem(f"sent{j}") for j in range(NB)]
        pool_made = sem("pool_made")
        waited = sem("waited")
        xvar_ready = sem("xvar_ready")
        avar_ready = sem("avar_ready")
        hvar_ready = sem("hvar_ready")
        xpow_done = sem("xpow_done")
        apow_done = sem("apow_done")
        hpow_done = sem("hpow_done")
        dve_chain = sem("dve_chain")
        f_step = sem("f_step")
        x_taken = sem("x_taken")
        xn_ready = sem("xn_ready")
        turned = sem("turned")
        copied = sem("copied")
        cols_ps = sem("cols_ps")
        cols_ready = sem("cols_ready")
        act_setup = sem("act_setup")
        mask_ready = sem("mask_ready")
        wqn_ready = sem("wqn_ready")
        nvd_ready = sem("nvd_ready")
        null_ps = sem("null_ps")
        nsn_ready = sem("nsn_ready")
        ctx_cur_ready = sem("ctx_cur_ready")
        side_ps = sem("side_ps")
        side_free = sem("side_free")
        proj_q = sem("proj_q")
        proj_k = sem("proj_k")
        proj_v = sem("proj_v")
        q_ready = sem("q_ready")
        k_ready = sem("k_ready")
        v_ready = sem("v_ready")
        scored = sem("scored")
        row_max = sem("row_max")
        nmax_ready = sem("nmax_ready")
        diff_ready = sem("diff_ready")
        null_exp_done = sem("null_exp_done")
        exp_done = sem("exp_done")
        denom_ready = sem("denom_ready")
        recip_ready = sem("recip_ready")
        probs_ready = sem("probs_ready")
        null_p_ready = sem("null_p_ready")
        probs_turned = sem("probs_turned")
        pT_lo = sem("pT_lo")
        pT_hi = sem("pT_hi")
        weighed = sem("weighed")
        oT_ready = sem("oT_ready")
        out_added = sem("out_added")
        null_turned = sem("null_turned")
        null_pT_ready = sem("null_pT_ready")
        acc_done = sem("acc_done")
        acc_free = sem("acc_free")
        stage_free = sem("stage_free")
        h2_ready = sem("h2_ready")
        df_ready = sem("df_ready")
        ex_ready = sem("ex_ready")
        onehot_ready = sem("onehot_ready")
        placed = sem("placed")
        early_ready = sem("early_ready")
        fill_ready = sem("fill_ready")
        tables_ready = sem("tables_ready")
        xn_s_ready = [sem(f"xn_s_ready{j}") for j in range(2)]
        xs_turned = [sem(f"xs_turned{j}") for j in range(2)]
        xsT_ready = [sem(f"xsT_ready{j}") for j in range(2)]
        h_ps = [sem(f"h_ps{j}") for j in range(2)]
        h_sb = [sem(f"h_sb{j}") for j in range(2)]
        y_ps = [sem(f"y_ps{j}") for j in range(2)]
        b1_ready = [sem(f"b1_ready{j}") for j in range(2)]
        y_added = sem("y_added")
        y_ready = [sem(f"y_ready{j}") for j in range(2)]

        def row_of(v, parts=P):
            return v.rearrange("(a n) -> a n", a=1).partition_broadcast(parts)

        def ctx_half(g, s):
            return ctx_split[0:CC, ds(g % 2, 1), s, :, :].rearrange("p a c n -> p (a c) n")

        def x_half(g, s):
            return x_split[:, ds(g % 2, 1), s, :, :].rearrange("p a k n -> p (a k) n")

        def tiles_used(engine):
            return engine.value_load(used_i[0:1, 0:1], min_val=NU, max_val=NS)

        def over(ap, axis, n):
            shape = list(ap.shape)
            shape.insert(axis, n)
            return ap.unsqueeze(axis).broadcast_to(shape)

        TURN_CTX = (0, 1)
        TURN_X = (2, 3)
        NULL_SCORES = 4
        TURN_H2 = (5, 6)
        LOGITS = 7
        COUNTS = 8
        NULL_OUT = 9
        FIRST_TASKS, TASKS, LAST_TASKS = 6, 9, 4

        def task(g, kind):
            if isinstance(g, int) and g == 0:
                return 5 if kind == NULL_OUT else kind
            if isinstance(g, int) and g >= NG - 1:
                return FIRST_TASKS + TASKS * (NG - 2) + LAST_TASKS * (g - NG + 1) + kind - TURN_H2[0]
            return (g - 1) * TASKS + FIRST_TASKS + kind

        def kind_of(hp, first, last):
            if first:
                return {0: 0, 1: 1, 2: 2, 3: 3, 4: NULL_SCORES, 6: NULL_OUT}.get(hp)
            if last:
                return {3: TURN_H2[0], 4: LOGITS, 5: COUNTS}.get(hp)
            return {0: 0, 1: 1, 2: 2, 3: 3, 4: NULL_SCORES, 5: TURN_H2[0], 6: LOGITS, 7: COUNTS}[hp]

        def second_kind_of(hp, first, last):
            return TURN_H2[1] if not first and hp == (3 if last else 5) else None

        N_ROWS, N_SMALL = 4, 5
        PARTS = ((0, 0), (0, 1), (1, 0))
        F_STEPS = 27
        block = ctx.enter_context(nc.Block())

        @block.sync
        def _(sp):
            def group(src, g):
                return src.rearrange("b p d -> p b d")[:, g * GT:(g + 1) * GT, :]

            sp.dma_start(x_sb[:, 0:GT, :], group(x, 0)).then_inc(x_in[0], 16)
            sp.dma_start(ctx_sb, group(ctx_in, 0)).then_inc(c_in, 16)
            w_kv_v = w_kv.rearrange("(c p) n -> p c n", p=CC)
            sp.dma_start(wq_sb, w_q.rearrange("(k p) n -> p k n", p=P)).then_inc(wq_in, 16)
            sp.dma_start(wk_sb[0:CC], w_kv_v[:, :, 0:INNER]).then_inc(wk_in, 16)
            sp.dma_start(wv_sb[0:CC], w_kv_v[:, :, INNER:2 * INNER]).then_inc(wv_in, 16)
            for g in range(1, NG):
                sp.dma_start(x_sb[:, g * GT:(g + 1) * GT, :], group(x, g)).then_inc(x_in[g], 16)
                if g == 1:
                    sp.wait_ge(turned, 2)
                    sp.dma_start(ctx_sb, group(ctx_in, 1)).then_inc(c_in, 16)
                    sp.dma_start(wout_sb[:, :, :], w_out.rearrange("(c p) n -> p c n", p=P)).then_inc(wout_in, 16)
            sp.wait_ge(pool_made, 18)
            sp.dma_start(rows_list[FILL:FILL + P, :], filling[:, :]).then_inc(filled, 16)

            for g in range(2, NG):
                sp.wait_ge(side_ps, task(g - 2, 1) + 1)
                sp.dma_start(ctx_sb, group(ctx_in, g)).then_inc(c_in, 16)

            w1_v = w_1.rearrange("e (k p) n -> e p k n", p=P)
            w2_v = w_2.rearrange("e (c p) n -> e p c n", p=P)


            def expert_of(i, j):
                return sp.value_load(eid_i[0:1, ds(i * NB + j, 1)], min_val=0, max_val=E - 1)

            def first_weights(e, i, j, reused=True):
                k = (i - 1) * 2 + j // 2
                if reused:
                    sp.wait_ge(h_ps[j % 2], 2 * k + 2)
                sp.dma_start(w1_sb[j], w1_v[ds(e, 1)].rearrange("a p k n -> p (a k) n")).then_inc(w1_in[j], 16)

            def second_weights(e, i, j, reused=True):
                k = (i - 1) * 2 + j // 2
                if reused:
                    sp.wait_ge(y_ps[j % 2], k + 1)
                sp.dma_start(w2_sb[j], w2_v[ds(e, 1)].rearrange("a p c n -> p (a c) n")).then_inc(w2_in[j], 16)
                if reused:
                    sp.wait_ge(y_ready[j % 2], k + 1)
                sp.dma_start(b2_sb[j], b_2[ds(e, 1), :].broadcast_to([P, D])).then_inc(b2_in[j], 16)

            def weights(i, j, reused=True):
                e = expert_of(i, j)
                first_weights(e, i, j, reused)
                second_weights(e, i, j, reused)

            def rows(i, j, reused=True):
                r = sp.value_load(row_i[0:1, ds(i * NB + j, 1)], min_val=0, max_val=FILL)
                if reused:
                    sp.wait_ge(sent[j], 16 * i)
                sp.dma_start(xs_sb[j], rows_list[ds(r, P), :]).then_inc(xs_in[j], 16)

            sp.wait_ge(early_ready, 1)
            sp.wait_ge(proj_v, NG * HP)
            for j in range(NB):
                weights(0, j, reused=False)
                if j == 0:
                    sp.wait_ge(listed, 16 * GT * (NG - 1))
                rows(0, j, reused=False)
            weights(1, 0)
            rows(1, 0)
            sp.wait_ge(fill_ready, 1)
            fill_rows = [sp.value_load(fill_i[0:1, e:e + 1], min_val=0, max_val=FILL - P) for e in range(E)]
            for r in fill_rows:
                sp.dma_start(rows_list[ds(r, P), :], filling[:, :]).then_inc(filled, 16)
            sp.wait_ge(tables_ready, 1)
            e = expert_of(1, 1)
            first_weights(e, 1, 1)
            sp.wait_ge(listed, 16 * B)
            sp.wait_ge(filled, 16 * (E + 1))
            rows(1, 1)
            second_weights(e, 1, 1)
            with sp.Fori(1, NU // NB - 1) as i:
                for ahead, j in ((0, 2), (0, 3), (1, 0), (1, 1)):
                    rows(i + ahead, j)
                    weights(i + ahead, j)
            for t in range(NU - 2, NU):
                rows(t // NB, t % NB)
                weights(t // NB, t % NB)
            used = tiles_used(sp)
            rows(NU // NB, NU % NB)
            for t in range(NU, NS):
                with sp.If(used > t):
                    weights(t // NB, t % NB)
                    if t + 1 < NS:
                        rows((t + 1) // NB, (t + 1) % NB)
            for j in range(NB):
                sp.wait_ge(sent[j], 16 * (NU // NB))
            for t in range(NU, NS):
                with sp.If(used > t):
                    sp.wait_ge(sent[t % NB], 16 * (t // NB + 1))

        @block.gpsimd
        def _(pool):
            made = [0]

            def make(ins):
                made[0] += 1
                ins.then_inc(pool_made, 1)
                pool.wait_ge(pool_made, made[0])

            def power_x(g):
                pool.wait_ge(xvar_ready, g + 1)
                mine = rstd_x[:, g * GT:(g + 1) * GT]
                pool.tensor_tensor(mine, mine, minus_half[:, :], ALU.pow).then_inc(xpow_done, 1)
                pool.wait_ge(xpow_done, g + 1)

            def power(rstd, ready, done, n):
                pool.wait_ge(ready, n)
                pool.tensor_tensor(rstd[:, :], rstd[:, :], minus_half[:, :], ALU.pow).then_inc(done, 1)
                pool.wait_ge(done, n)

            make(pool.memset(as_rows[:, :], 0.0))
            make(pool.memset(minus_half[:, :], -0.5))
            make(pool.memset(ident[:, :], 0.0))
            make(pool.affine_select(out=ident[:, :], in_=ident[:, :], compare_op=ALU.not_equal, fill=1.0,
                                    base=0, pattern=[[-1, P]], channel_multiplier=1))
            power_x(0)
            make(pool.memset(kT, 0.0))
            make(pool.memset(row0_one[:, :], 0.0))
            make(pool.memset(row0_one[0:1, :], 1.0))
            make(pool.memset(mask_bias[:, :, :], 0.0))
            make(pool.memset(null_p[:, :], 0.0))
            make(pool.memset(nv_diag[:, :, :], 0.0))
            for half in range(2):
                v = nv_diag[half * DH:(half + 1) * DH].rearrange("p c (b h) -> p c b h", h=H)
                make(pool.affine_select(out=v, in_=v, compare_op=ALU.not_equal, fill=1.0, base=-half,
                                        pattern=[[-2, HP], [0, P // H], [1, H]], channel_multiplier=0))
            make(pool.memset(rows_of[:, :], 1.0))
            make(pool.affine_select(out=rows_of[:, :], in_=rows_of[:, :], compare_op=ALU.is_ge, fill=0.0,
                                    base=0, pattern=[[-H, GT]], channel_multiplier=1))
            make(pool.affine_select(out=rows_of[:, :], in_=rows_of[:, :], compare_op=ALU.is_ge, fill=0.0,
                                    base=H - 1, pattern=[[H, GT]], channel_multiplier=-1))
            make(pool.memset(filling[:, :], 0.0))
            make(pool.iota(token_i[:, :], [[P, B]], base=0, channel_multiplier=1))
            make(pool.iota(filling[:, TOKEN:TOKEN + 1].bitcast(I32), [[1, 1]], base=NO_TOKEN,
                           channel_multiplier=0))
            make(pool.memset(ones_bf[:, :], 1.0))
            make(pool.memset(before[:, :], 1.0))
            make(pool.affine_select(out=before[:, :], in_=before[:, :], compare_op=ALU.is_ge, fill=0.0,
                                    base=-1, pattern=[[1, P]], channel_multiplier=-1))
            make(pool.iota(iota_i[:, :], [[1, NS]], base=0, channel_multiplier=0))
            make(pool.memset(ones_e[:, :], 1.0))
            make(pool.memset(taken[:, :], 0.0))
            make(pool.memset(keep_scan[:, :, :], 1.0))
            make(pool.memset(keep_scan[:, :, 0:1], 0.0))
            pool.sem_inc(stage_free, 1)

            def next_context(g):
                pool.wait_ge(proj_v, (g + 1) * HP)
                pool.wait_ge(side_free, task(g, 1) + 1)
                pool.sem_inc(waited, 1)
                pool.tensor_copy(ctx_cur[0:CC], ctx_next[0:CC]).then_inc(ctx_cur_ready, 1)

            def list_rows(last):
                pool.wait_ge(placed, last + 1)
                pool.sem_inc(waited, 1)
                for b in range(GT):
                    pool.indirect_dma_start(
                        out=rows_list, out_offset=bass.IndirectOffsetOnAxis(ap=pos_i[:, b:b + 1], axis=0),
                        in_=stage[:, b, :], in_offset=None).then_inc(listed, 16)
                pool.wait_ge(listed, 16 * GT * (last + 1))
                pool.sem_inc(stage_free, 1)

            def group(g, first=False, last=False):
                if not first:
                    power(rstd_a, avar_ready, apow_done, g)
                if first:
                    for later in range(1, NG):
                        power_x(later)
                if not first:
                    power(rstd_h, hvar_ready, hpow_done, g)
                if not last:
                    next_context(g)
                if not first:
                    list_rows(g - 1)

            group(0, first=True)
            with pool.Fori(1, NG - 1) as g:
                group(g)
            group(NG - 1, last=True)
            def send(i, j):
                pool.wait_ge(y_ready[j % 2], i * 2 + j // 2 + 1)
                pool.sem_inc(waited, 1)
                pool.indirect_dma_start(
                    out=out.rearrange("b p d -> (b p) d"),
                    out_offset=bass.IndirectOffsetOnAxis(ap=xs_sb[j][:, TOKEN:TOKEN + 1].bitcast(I32), axis=0),
                    in_=y_sb[j], in_offset=None, bounds_check=B * P - 1, oob_is_err=False).then_inc(sent[j], 16)

            power(rstd_a, avar_ready, apow_done, NG)
            send(0, 0)
            power(rstd_h, hvar_ready, hpow_done, NG)
            send(0, 1)
            send(0, 2)
            list_rows(NG - 1)
            send(0, 3)
            send(1, 0)
            with pool.Fori(1, NU // NB - 1) as i:
                for ahead, j in ((0, 1), (0, 2), (0, 3), (1, 0)):
                    send(i + ahead, j)
            for t in range(NU - 3, NU):
                send(t // NB, t % NB)
            pool.wait_ge(tables_ready, 1)
            used = tiles_used(pool)
            for t in range(NU, NS):
                with pool.If(used > t):
                    send(t // NB, t % NB)

        @block.tensor
        def _(pe):
            first_banks = [ps_s[:, 0:512], ps_s[:, 512:1024], ps_acc[:, 0:512], ps_acc[:, 512:1024]]
            pe.wait_ge(pool_made, 4)

            def turn_x(bank, k):
                for b in range(GT):
                    ins = pe.transpose(bank[:, b * P:(b + 1) * P], xn_cur[:, b, k * P:(k + 1) * P], ident[:, :])
                return ins

            def keep_busy(columns, times):
                for _ in range(times):
                    pe.matmul(ps_side[:, 0:columns.shape[-1]], ident[:, :], columns, start=True, stop=True)

            keep_busy(ident[:, :], 16)
            for c in range(2):
                pe.wait_ge(c_in, 16)
                for b in range(GT):
                    ins = pe.transpose(first_banks[c][0:CC, b * P:(b + 1) * P],
                                       ctx_sb[:, b, c * CC:(c + 1) * CC], ident[:, :])
                ins.then_inc(turned, 1)
            for k in range(KD):
                pe.wait_ge(xn_ready, 1)
                turn_x(first_banks[2 + k], k).then_inc(turned, 1)
            x_columns = xn_cur[:, 0:2, :].rearrange("p b d -> p (b d)")
            keep_busy(x_columns, 2)
            pe.wait_ge(rows_in, 16 * N_ROWS)
            pe.transpose(ps_o[:, 0:P], as_rows[:, :], ident[:, :]).then_inc(cols_ps, 1)

            def project_k(g, hp):
                if hp == 0:
                    pe.wait_ge(ctx_split_ready, g + 1)
                cols = slice(hp * P, (hp + 1) * P)
                for i, (w, t) in enumerate(PARTS):
                    for c in range(2):
                        ins = pe.matmul(ps_k[:, :], wk_split[0:CC, w, c, cols], ctx_half(g, t)[:, c, :],
                                        start=(i == 0 and c == 0), stop=(i == 2 and c == 1))
                ins.then_inc(proj_k, 1)

            def project_q(g, hp):
                if hp == 0:
                    pe.wait_ge(x_split_ready, g + 1)
                cols = slice(hp * P, (hp + 1) * P)
                for i, (w, t) in enumerate(PARTS):
                    for k in range(KD):
                        ins = pe.matmul(ps_qv[:, :], wq_split[:, w, k, cols], x_half(g, t)[:, k, :],
                                        start=(i == 0 and k == 0), stop=(i == 2 and k == KD - 1))
                ins.then_inc(proj_q, 1)

            def project_v(g, hp):
                pe.wait_ge(q_ready, g * HP + hp + 1)
                if hp == 0:
                    pe.wait_ge(ctx_cur_ready, g + 1)
                for b in range(GT):
                    for c in range(2):
                        ins = pe.matmul(ps_qv[:, b * P:(b + 1) * P], ctx_cur[0:CC, c, b * P:(b + 1) * P],
                                        wv_sb[0:CC, c, hp * P:(hp + 1) * P],
                                        start=(c == 0), stop=(c == 1))
                ins.then_inc(proj_v, 1)

            def project(g, hp):
                pe.wait_ge(v_ready, g * HP + hp)
                project_q(g, hp)
                project_k(g, hp)
                project_v(g, hp)

            def null_scores(xt, bank):
                for b in range(GT):
                    for k in range(KD):
                        ins = pe.matmul(bank[:, b * H:(b + 1) * H], xt[:, k, b * P:(b + 1) * P], wqn[:, k, :],
                                        start=(k == 0), stop=(k == KD - 1))
                return ins

            def add_out(g, hp):
                pe.wait_ge(oT_ready, g * HP + hp + 1)
                if hp == 0:
                    pe.wait_ge(acc_free, g)
                for b in range(GT):
                    ins = pe.matmul(ps_acc[:, b * D:(b + 1) * D], oT[:, b * P:(b + 1) * P], wout_sb[:, hp, :],
                                    start=(hp == 0 and b % 2 == 0), stop=False, skip_group_check=True)
                ins.then_inc(out_added, 1)

            def side(g, kind, first=False):
                if kind is None:
                    return
                own_bank = isinstance(g, int) and g == NG and kind == TURN_H2[1]
                bank = ps_o if own_bank else ps_side
                if not (first and kind == 0) and not own_bank:
                    pe.wait_ge(side_free, task(g, kind))
                if kind in TURN_CTX:
                    pe.wait_ge(c_in, 16 * (g + 2))
                    for b in range(GT):
                        ins = pe.transpose(ps_side[0:CC, b * P:(b + 1) * P],
                                           ctx_sb[:, b, kind * CC:(kind + 1) * CC], ident[:, :])
                elif kind in TURN_X:
                    pe.wait_ge(xn_ready, g + 2)
                    ins = turn_x(ps_side, kind - TURN_X[0])
                elif kind == NULL_SCORES:
                    ins = null_scores(xT_next, ps_side)
                elif kind == NULL_OUT:
                    pe.wait_ge(nvd_ready, 1)
                    for c in range(HP):
                        ins = pe.matmul(ps_side[:, 0:D], nv_diag[:, c, :], wout_sb[:, c, :],
                                        start=(c == 0), stop=(c == HP - 1))
                elif kind in TURN_H2:
                    k = kind - TURN_H2[0]
                    pe.wait_ge(h2_ready, g)
                    for b in range(GT):
                        ins = pe.transpose(bank[:, b * P:(b + 1) * P], h2[:, b, k * P:(k + 1) * P], ident[:, :])
                elif kind == LOGITS:
                    for b in range(GT):
                        for k in range(KD):
                            ins = pe.matmul(ps_side[:, b * E:(b + 1) * E], h2T[:, k, b * P:(b + 1) * P],
                                            wr_sb[:, k, :], start=(k == 0), stop=(k == KD - 1))
                elif kind == COUNTS:
                    pe.wait_ge(onehot_ready, g)
                    pe.matmul(ps_side[:, 0:GT * E], before[:, :], onehot[:, :, :], start=True, stop=True)
                    ins = pe.matmul(ps_side[:, P:P + GT * E], ones_bf[:, :],
                                    onehot[:, :, :].rearrange("p t e -> p e t"), start=True, stop=True)
                ins.then_inc(side_ps, 1)

            def turn_rows(i, j):
                par, k = j % 2, i * 2 + j // 2
                pe.wait_ge(xn_s_ready[par], k + 1)
                pe.wait_ge(y_ready[par], k)
                for c in range(KD):
                    ins = pe.transpose(ps_x[par][:, c * P:(c + 1) * P],
                                       xn_s[par][:, c * P:(c + 1) * P], ident[:, :])
                ins.then_inc(xs_turned[par], 1)

            def turn_null(g):
                pe.wait_ge(oT_ready, g * HP + HP)
                pe.wait_ge(null_p_ready, 2 * HP * (g + 1))
                pe.transpose(ps_o[:, 0:P], null_p[:, :], ident[:, :]).then_inc(null_turned, 1)

            def add_null(g):
                pe.wait_ge(null_pT_ready, g + 1)
                if isinstance(g, int) and g < NG - 1:
                    pe.wait_ge(side_free, FIRST_TASKS)
                for b in range(GT):
                    ins = pe.matmul(ps_acc[:, b * D:(b + 1) * D], null_pT[:, :], nw_rows[:, b, :],
                                    start=False, stop=True, skip_group_check=True)
                ins.then_inc(acc_done, 1)

            def group(g, first=False, last=False):
                for hp in range(HP):
                    n = g * HP + hp
                    pe.wait_ge(q_ready, n + 1)
                    pe.wait_ge(k_ready, 2 * n + 2)
                    for half in range(2):
                        if not (first and hp == 0):
                            pe.wait_ge(pT_hi if half else pT_lo, n)
                        bias = mask_bias[:, ds(g * GT + 2 * half, 2), :].unsqueeze(2).broadcast_to([P, 2, 2, P])
                        pe.matmul(ps_s[:, half * 512:(half + 1) * 512], row0_one[:, :], bias,
                                  start=True, stop=False, skip_group_check=True)
                        for b in (2 * half, 2 * half + 1):
                            ins = pe.matmul(ps_s[:, b * 2 * P:(b + 1) * 2 * P], qT[:, b * P:(b + 1) * P],
                                            kT[:, b, :], start=False, stop=True, skip_group_check=True)
                        ins.then_inc(scored, 1)
                    if hp == 0 and not first:
                        turn_null(g - 1)
                    if hp + 1 < HP:
                        project(g, hp + 1)
                    elif not last:
                        project(g + 1, 0)
                    side(g, kind_of(hp, first, last), first)
                    for half in range(2):
                        pe.wait_ge(probs_ready, 2 * n + half + 1)
                        for j in range(GT * half, GT * half + GT):
                            ins = pe.transpose(ps_s[:, j * P:(j + 1) * P], probs[:, j, :], ident[:, :])
                        ins.then_inc(probs_turned, 1)
                    if hp > 0:
                        if first and hp == 1:
                            pe.wait_ge(wout_in, 16)
                        add_out(g, hp - 1)
                    elif not first:
                        add_out(g - 1, HP - 1)
                        add_null(g - 1)
                    pe.wait_ge(v_ready, n + 1)
                    if hp == 0 and not first:
                        pe.wait_ge(null_pT_ready, g)
                    if not (first and hp == 0):
                        pe.wait_ge(oT_ready, n)
                    for b in range(GT):
                        if b == 0:
                            pe.wait_ge(pT_lo, n + 1)
                        if b == GT // 2:
                            pe.wait_ge(pT_hi, n + 1)
                        for h in range(2):
                            ins = pe.matmul(ps_o[h * DH:(h + 1) * DH, b * P:(b + 1) * P],
                                            v_sb[hp % 2][:, b, h * DH:(h + 1) * DH], probsT[:, 2 * b + h, :],
                                            start=True, stop=True, skip_group_check=True)
                    ins.then_inc(weighed, 1)
                    side(g, second_kind_of(hp, first, last), first)
            keep_busy(x_columns, 2)
            pe.wait_ge(w_low, 2)
            project_k(0, 0)
            keep_busy(x_columns, 3)
            pe.wait_ge(w_low, 4)
            project_q(0, 0)
            pe.wait_ge(wv_in, 16)
            project_v(0, 0)
            pe.wait_ge(copied, 4)
            pe.wait_ge(wqn_ready, 1)
            null_scores(xT_next, ps_o).then_inc(null_ps, 1)
            pe.wait_ge(mask_ready, 1)
            pe.wait_ge(pool_made, 9)
            group(0, first=True)
            with pe.Fori(1, NG - 1) as g:
                group(g)
            group(NG - 1, last=True)
            turn_rows(0, 0)
            turn_null(NG - 1)
            add_out(NG - 1, HP - 1)
            add_null(NG - 1)

            def turn_next(i, j):
                if j + 1 < NB:
                    turn_rows(i, j + 1)
                else:
                    turn_rows(i + 1, 0)

            def hidden(i, j):
                par, k = j % 2, i * 2 + j // 2
                pe.wait_ge(w1_in[j], 16 * (i + 1))
                pe.wait_ge(xsT_ready[par], k + 1)
                pe.wait_ge(h_sb[par], FC * k)
                for f in range(FC):
                    for c in range(KD):
                        ins = pe.matmul(ps_h[par][:, f * P:(f + 1) * P], w1_sb[j][:, c, f * P:(f + 1) * P],
                                        xsT[par][:, c, :], start=(c == 0), stop=(c == KD - 1))
                    if f % 4 == 3:
                        ins.then_inc(h_ps[par], 1)

            def outputs(i, j):
                par, k = j % 2, i * 2 + j // 2
                pe.wait_ge(w2_in[j], 16 * (i + 1))
                for f in range(FC):
                    pe.wait_ge(h_sb[par], FC * k + f + 1)
                    ins = pe.matmul(ps_y[par], hT[par][:, f, :], w2_sb[j][:, f, :],
                                    start=(f == 0), stop=(f == FC - 1))
                ins.then_inc(y_ps[par], 1)

            def tile(i, j):
                hidden(i, j)
                turn_next(i, j)
                outputs(i, j)

            tile(0, 0)
            pe.wait_ge(acc_free, NG)
            hidden(0, 1)
            turn_next(0, 1)
            outputs(0, 1)
            side(NG, TURN_H2[0])
            side(NG, TURN_H2[1])
            side(NG, LOGITS)
            hidden(0, 2)
            side(NG, COUNTS)
            turn_next(0, 2)
            outputs(0, 2)
            tile(0, 3)
            hidden(1, 0)
            outputs(1, 0)
            turn_next(1, 0)
            with pe.Fori(1, NU // NB - 1) as i:
                for ahead, j in ((0, 1), (0, 2), (0, 3), (1, 0)):
                    tile(i + ahead, j)
            for t in range(NU - 3, NU):
                tile(t // NB, t % NB)
            pe.wait_ge(tables_ready, 1)
            used = tiles_used(pe)
            for t in range(NU, NS):
                with pe.If(used > t):
                    hidden(t // NB, t % NB)
                    if t + 1 < NS:
                        turn_next(t // NB, t % NB)
                    outputs(t // NB, t % NB)

        @block.scalar
        def _(act):
            act.dma_start(nk_row[:, :], null_kv[0:1, :].broadcast_to([P, DH])).then_inc(nk_in, 16)
            act.wait_ge(pool_made, 2)
            act.dma_start(as_rows[0:E * FC, :], b_1.rearrange("e (c p) -> (e c) p", p=P)).then_inc(rows_in, 16)
            act.dma_start(as_rows[E * FC:E * FC + KD, :], g_norm.rearrange("(k p) -> k p", p=P)).then_inc(rows_in, 16)
            for half in range(2):
                act.dma_start(as_rows[E * FC + KD:E * FC + KD + 1, half * DH:(half + 1) * DH],
                              null_kv[1:2, :]).then_inc(rows_in, 16)
            act.dma_start(mask_u8[:, :], mask.rearrange("b n -> (b n)").rearrange("(a n) -> a n", a=1)
                          ).then_inc(small_in, 16)
            act.dma_start(gates[:, 0:1], row_of(g_xattn)).then_inc(small_in, 16)
            act.dma_start(gates[:, 1:2], row_of(g_ffn)).then_inc(small_in, 16)
            act.dma_start(gout_row[:, :], row_of(g_out)).then_inc(small_in, 16)
            act.dma_start(wr_sb[:, :, :], w_r.rearrange("(k p) e -> p k e", p=P)).then_inc(small_in, 16)
            act.activation(warm[:, :], minus_half[:, 0:1], ACT.Exp)
            first_banks = [ps_s[:, 0:512], ps_s[:, 512:1024], ps_acc[:, 0:512], ps_acc[:, 512:1024]]
            for c in range(2):
                act.wait_ge(turned, c + 1)
                ins = act.activation(ctx_cur[0:CC, c, :], first_banks[c][0:CC], ACT.Copy)
                if c == 1:
                    ins.then_inc(ctx_cur_ready, 1)
                act.activation(ctx_half(0, 0)[:, c, :], first_banks[c][0:CC], ACT.Copy).then_inc(copied, 1)
            act.wait_ge(wk_in, 16)
            for c in range(2):
                act.activation(wk_split[0:CC, 0, c, :], wk_sb[0:CC, c, :], ACT.Copy).then_inc(w_high, 1)
            act.wait_ge(wq_in, 16)
            for k in range(KD):
                act.activation(wq_split[:, 0, k, :], wq_sb[:, k, :], ACT.Copy).then_inc(w_high, 1)
            act.wait_ge(cols_ps, 1)
            act.activation(as_cols[:, :], ps_o[:, 0:P], ACT.Copy).then_inc(cols_ready, 1)
            act.wait_ge(cols_ready, 1)
            for k in range(KD):
                act.wait_ge(turned, 3 + k)
                act.activation(xT_next[:, k, :], first_banks[2 + k], ACT.Copy, scale=gn_col[:, k:k + 1])
                act.activation(x_half(0, 0)[:, k, :], first_banks[2 + k], ACT.Copy, scale=gn_col[:, k:k + 1]
                               ).then_inc(copied, 1)

            def take_q(n, first_unit=False):
                act.wait_ge(proj_q, n + 1)
                if not first_unit:
                    act.wait_ge(scored, 2 * n)
                act.activation(qT, ps_qv[:, :], ACT.Copy).then_inc(q_ready, 1)

            def side(g, kind):
                if kind is None:
                    return
                if kind in TURN_CTX + TURN_X + TURN_H2:
                    act.wait_ge(side_ps, task(g, kind) + 1)
                if kind == 0:
                    act.wait_ge(ctx_cur_ready, g + 1)
                if kind in TURN_CTX:
                    act.activation(ctx_next[0:CC, kind, :], ps_side[0:CC], ACT.Copy)
                    act.activation(ctx_half(g + 1, 0)[:, kind, :], ps_side[0:CC], ACT.Copy
                                   ).then_inc(side_free, 1)
                elif kind in TURN_X:
                    k = kind - TURN_X[0]
                    act.activation(xT_next[:, k, :], ps_side[:, :], ACT.Copy, scale=gn_col[:, k:k + 1])
                    act.activation(x_half(g + 1, 0)[:, k, :], ps_side[:, :], ACT.Copy, scale=gn_col[:, k:k + 1]
                                   ).then_inc(side_free, 1)
                elif kind in TURN_H2:
                    bank = ps_o if isinstance(g, int) and g == NG and kind == TURN_H2[1] else ps_side
                    act.activation(h2T[:, kind - TURN_H2[0], :], bank[:, :], ACT.Copy).then_inc(side_free, 1)
                elif kind == LOGITS:
                    act.wait_ge(df_ready, g)
                    act.activation(r_b[:, :, :], r_a[:, :, :], ACT.Exp).then_inc(ex_ready, 1)

            def take_null(g):
                act.wait_ge(null_turned, g + 1)
                act.activation(null_pT[:, :], ps_o[:, 0:P], ACT.Copy).then_inc(null_pT_ready, 1)

            def group(g, first=False, last=False):
                for hp in range(HP):
                    n = g * HP + hp
                    if hp == 0 and not first:
                        take_null(g - 1)
                    for half in range(2):
                        m, b2 = 2 * n + half, slice(2 * half, 2 * half + 2)
                        act.wait_ge(nmax_ready, m + 1)
                        if not (first and hp == 0):
                            act.wait_ge(probs_turned, m - 1)
                        for j in range(GT * half, GT * half + GT):
                            ins = act.activation(probs[:, j, :], ps_s[:, j * P:(j + 1) * P], ACT.Exp,
                                                 bias=nmax[:, j // 2, j % 2:j % 2 + 1], scale=SCALE,
                                                 accum_out=sums[:, j // 2, j % 2:j % 2 + 1])
                            if j % GT == 1:
                                act.wait_ge(diff_ready, m + 1)
                                act.activation(null_exp[:, b2, :], null_diff[:, b2, :], ACT.Exp
                                               ).then_inc(null_exp_done, 1)
                        ins.then_inc(exp_done, 1)
                        if half == 0 and (hp + 1 < HP or not last):
                            take_q(n + 1)
                    kind = kind_of(hp, first, last)
                    if kind != LOGITS:
                        side(g, kind)
                    act.wait_ge(probs_turned, 2 * n + 1)
                    if not (first and hp == 0):
                        act.wait_ge(weighed, n)
                    act.activation(probsT[:, 0:GT, :], ps_s[:, 0:512].rearrange("p (j n) -> p j n", j=GT),
                                   ACT.Copy).then_inc(pT_lo, 1)
                    act.wait_ge(weighed, n + 1)
                    if not (first and hp == 0):
                        act.wait_ge(out_added, n)
                    act.activation(oT, ps_o[:, :], ACT.Copy).then_inc(oT_ready, 1)
                    if kind == LOGITS:
                        side(g, kind)
                    side(g, second_kind_of(hp, first, last))

            take_q(0, first_unit=True)
            act.wait_ge(small_in, 16 * N_SMALL)
            act.activation(tanhs[:, :], gates[:, :], ACT.Tanh).then_inc(act_setup, 1)
            group(0, first=True)
            with act.Fori(1, NG - 1) as g:
                group(g)
            group(NG - 1, last=True)
            take_null(NG - 1)

            def tile(i, j):
                par, k = j % 2, i * 2 + j // 2
                act.wait_ge(b1_ready[par], k + 1)
                act.wait_ge(y_ps[par], k)
                for f in range(FC):
                    if f % 4 == 0:
                        act.wait_ge(h_ps[par], 2 * k + f // 4 + 1)
                    act.activation(hT[par][:, f, :], ps_h[par][:, f * P:(f + 1) * P], ACT.Gelu,
                                   bias=b1_cur[par][:, f:f + 1]).then_inc(h_sb[par], 1)

            tile(0, 0)
            tile(0, 1)
            side(NG, TURN_H2[0])
            side(NG, TURN_H2[1])
            side(NG, LOGITS)
            tile(0, 2)
            tile(0, 3)
            tile(1, 0)
            with act.Fori(1, NU // NB - 1) as i:
                for ahead, j in ((0, 1), (0, 2), (0, 3), (1, 0)):
                    tile(i + ahead, j)
            for t in range(NU - 3, NU):
                tile(t // NB, t % NB)
            act.wait_ge(tables_ready, 1)
            used = tiles_used(act)
            for t in range(NU, NS):
                with act.If(used > t):
                    tile(t // NB, t % NB)

        @block.vector
        def _(dve):
            chained = [0]

            def link(ins):
                chained[0] += 1
                ins.then_inc(dve_chain, 1)
                dve.wait_ge(dve_chain, chained[0])

            def statistics(src, step, mv, rstd, scale, shift, ready):
                for b in range(GT):
                    ins = dve.bn_stats(stats[:, b, :], src(b))
                step(ins)
                dve.sem_inc(waited, 1)
                for b in range(GT):
                    ins = dve.bn_aggr(mv[:, b, :], stats[:, b, :])
                step(ins)
                dve.tensor_scalar(rstd, mv[:, :, 1], scale, shift, ALU.mult, ALU.add).then_inc(ready, 1)

            def x_rows(g, b):
                return x_sb[:, ds(g * GT + b, 1), :].rearrange("p a d -> p (a d)")

            def stats_x(g):
                mine = slice(g * GT, (g + 1) * GT)
                dve.wait_ge(x_in[g], 16)
                statistics(lambda b: x_sb[:, g * GT + b, :], link, mv_x[:, mine, :], rstd_x[:, mine],
                           1.0 + EPS, EPS * EPS, xvar_ready)

            def norm_x(g):
                dve.wait_ge(xpow_done, g + 1)
                dve.tensor_copy(mean_cur[:, :], mv_x[:, ds(g * GT, GT), 0:1].rearrange("p b c -> p (b c)"))
                dve.tensor_copy(rstd_cur[:, :], rstd_x[:, ds(g * GT, GT)]).then_inc(x_taken, 1)
                dve.wait_ge(x_taken, g + 1)
                for b in range(GT):
                    ins = dve.tensor_scalar(xn_cur[:, b, :], x_rows(g, b), mean_cur[:, b:b + 1],
                                            rstd_cur[:, b:b + 1], ALU.subtract, ALU.mult)
                ins.then_inc(xn_ready, 1)

            def context_low(g, full):
                dve.tensor_tensor(ctx_half(g, 1), full[0:CC], ctx_half(g, 0), ALU.subtract
                                  ).then_inc(ctx_split_ready, 1)

            def x_low(g):
                dve.tensor_tensor(x_half(g, 1), xT_next[:, :, :], x_half(g, 0), ALU.subtract
                                  ).then_inc(x_split_ready, 1)

            def take_k(n, first_unit=False):
                dve.wait_ge(proj_k, n + 1)
                if not first_unit:
                    dve.wait_ge(scored, 2 * n)
                for h in range(2):
                    p = slice(h * DH, (h + 1) * DH)
                    dve.tensor_copy(kT[p, :, h * P:(h + 1) * P], ps_k[p, :].rearrange("p (b n) -> p b n", b=GT)
                                    ).then_inc(k_ready, 1)

            def take_v(n, par, early=False):
                dve.wait_ge(proj_v, n + 1)
                if not early:
                    dve.wait_ge(weighed, n - 1)
                dve.tensor_copy(v_sb[par], ps_qv[:, :].rearrange("p (b n) -> p b n", b=GT)).then_inc(v_ready, 1)

            def take_null_scores(g, bank):
                ins = dve.tensor_scalar(nsn[:, ds(g * GT, GT), :].rearrange("p b h -> p (b h)"), bank, -SCALE,
                                        None, ALU.mult)
                ins.then_inc(nsn_ready, 1)

            stats_x(0)
            norm_x(0)
            dve.wait_ge(nk_in, 16)
            dve.wait_ge(wq_in, 16)
            link(dve.tensor_tensor(nk_prod, wq_sb.rearrange("p k (h d) -> p (k h) d", h=H),
                                   over(nk_row[:, :], 1, KD * H), ALU.mult))
            dve.wait_ge(copied, 2)
            context_low(0, ctx_cur)
            for c in range(2):
                dve.wait_ge(w_high, c + 1)
                dve.tensor_tensor(wk_split[0:CC, 1, c, :], wk_sb[0:CC, c, :], wk_split[0:CC, 0, c, :], ALU.subtract
                                  ).then_inc(w_low, 1)
            for k in range(KD):
                dve.wait_ge(w_high, 3 + k)
                dve.tensor_tensor(wq_split[:, 1, k, :], wq_sb[:, k, :], wq_split[:, 0, k, :], ALU.subtract
                                  ).then_inc(w_low, 1)
            dve.wait_ge(copied, 4)
            x_low(0)
            dve.tensor_reduce(wqn[:, :, :].rearrange("p k h -> p (k h)"), nk_prod, AX_X, ALU.add
                              ).then_inc(wqn_ready, 1)
            dve.wait_ge(pool_made, 5)
            take_k(0, first_unit=True)
            dve.wait_ge(small_in, 16 * N_SMALL)
            dve.wait_ge(pool_made, 8)
            dve.tensor_scalar(mask_bias[0:1, :, :].rearrange("p b n -> p (b n)"), mask_u8[:, :], -1.0, MASKED,
                              ALU.add, ALU.mult).then_inc(mask_ready, 1)
            take_v(0, 0, early=True)
            dve.wait_ge(null_ps, 1)
            take_null_scores(0, ps_o[:, 0:GT * H])
            dve.wait_ge(nsn_ready, 1)

            def later_constants():
                dve.wait_ge(cols_ready, 1)
                dve.wait_ge(pool_made, 26)
                dve.tensor_scalar(nv_diag[:, :, :], nv_diag[:, :, :], nv_col[:, 0:1], None, ALU.mult
                                  ).then_inc(nvd_ready, 1)
                dve.wait_ge(act_setup, 1)
                link(dve.tensor_scalar(gout_row[:, :], gout_row[:, :], tanhs[:, 0:1], None, ALU.mult))
                link(dve.tensor_copy(iota_s[:, :], iota_i[:, :]))
                link(dve.tensor_scalar(iota_e8[:, :], iota_s[:, 0:E], float(-E), None, ALU.add))
                link(dve.tensor_scalar(region[:, :], iota_s[:, 0:E], float(CAP), None, ALU.mult))

            count = [0]

            def router(last, part):
                def step(ins):
                    count[0] += 1
                    ins.then_inc(f_step, 1)
                    dve.wait_ge(f_step, last * F_STEPS + count[0])

                x2 = stage[:, :, 0:D]
                if part == 0:
                    count[0] = 0
                    statistics(lambda b: att_cur[:, b, :], step, mv_a, rstd_a[:, :], 1.0, EPS, avar_ready)
                elif part == 1:
                    for b in range(GT):
                        ins = dve.scalar_tensor_tensor(out=att_cur[:, b, :], in0=att_cur[:, b, :],
                                                       scalar=mv_a[:, b, 0:1], in1=gout_row[:, :],
                                                       op0=ALU.subtract, op1=ALU.mult)
                    step(ins)
                elif part == 2:
                    dve.wait_ge(apow_done, last + 1)
                    dve.wait_ge(stage_free, last + 1)
                    for b in range(GT):
                        ins = dve.scalar_tensor_tensor(out=x2[:, b, :], in0=att_cur[:, b, :],
                                                       scalar=rstd_a[:, b:b + 1], in1=x_rows(last, b),
                                                       op0=ALU.mult, op1=ALU.add)
                    step(ins)
                elif part == 3:
                    statistics(lambda b: x2[:, b, :], step, mv_h, rstd_h[:, :], 1.0, EPS, hvar_ready)
                elif part == 4:
                    dve.wait_ge(hpow_done, last + 1)
                    for b in range(GT):
                        ins = dve.tensor_scalar(h2[:, b, :], x2[:, b, :], mv_h[:, b, 0:1], rstd_h[:, b:b + 1],
                                                ALU.subtract, ALU.mult)
                    ins.then_inc(h2_ready, 1)
                    step(dve.tensor_copy(stage[:, :, MEAN:MEAN + 1], mv_h[:, :, 0:1]))
                    step(dve.tensor_copy(stage[:, :, RSTD:RSTD + 1].rearrange("p b a -> p (b a)"), rstd_h[:, :]))
                    step(dve.tensor_copy(stage[:, :, TOKEN:TOKEN + 1].bitcast(I32).rearrange("p b a -> p (b a)"),
                                         token_i[:, ds(last * GT, GT)]))
                elif part == 6:
                    flat = "p t e -> p (t e)"
                    step(dve.tensor_copy(logits[:, :, :].rearrange(flat), ps_side[:, 0:GT * E]))
                    step(dve.tensor_reduce(r_max[:, :], logits[:, :, :], AX_X, ALU.max))
                    largest = over(r_max[:, :], 2, E)
                    dve.tensor_tensor(r_a[:, :, :], logits[:, :, :], largest, ALU.subtract).then_inc(df_ready, 1)
                    step(dve.tensor_tensor(logits[:, :, :], logits[:, :, :], largest, ALU.is_equal))
                    step(dve.tensor_tensor(logits[:, :, :], logits[:, :, :], over(iota_e8[:, :], 1, GT), ALU.mult))
                    step(dve.tensor_reduce(first_e[:, :], logits[:, :, :], AX_X, ALU.min))
                    dve.tensor_tensor(onehot[:, :, :], over(iota_e8[:, :], 1, GT), over(first_e[:, :], 2, E),
                                      ALU.is_equal).then_inc(onehot_ready, 1)
                elif part == 7:
                    dve.wait_ge(ex_ready, last + 1)
                    step(dve.tensor_reduce(r_sum[:, :], r_b[:, :, :], AX_X, ALU.add))
                    step(dve.reciprocal(r_max[:, :], r_sum[:, :]))
                    step(dve.tensor_scalar(stage[:, :, COEF:COEF + 1].rearrange("p b a -> p (b a)"), r_max[:, :],
                                           tanhs[:, 1:2], None, ALU.mult))
                    flat = "p e t -> p (e t)"
                    dve.wait_ge(side_ps, task(last + 1, COUNTS) + 1)
                    step(dve.tensor_copy(counts[:, :, :].rearrange(flat), ps_side[:, P:P + GT * E]))
                    step(dve.tensor_tensor_scan(upto[:, :, :].rearrange(flat), keep_scan[:, :, :].rearrange(flat),
                                                counts[:, :, :].rearrange(flat), 0.0, ALU.mult, ALU.add))
                    step(dve.tensor_tensor(base[:, :, :], upto[:, :, :], counts[:, :, :], ALU.subtract))
                    step(dve.tensor_tensor(base[:, :, :], base[:, :, :], over(taken[:, :], 2, GT), ALU.add))
                    step(dve.tensor_tensor(base[:, :, :], base[:, :, :], over(region[:, :], 2, GT), ALU.add))
                    step(dve.tensor_tensor(r_a[:, :, :], ps_side[:, 0:GT * E].rearrange("p (t e) -> p t e", e=E),
                                           base[:, :, :].rearrange("p e t -> p t e"), ALU.add))
                    dve.sem_inc(side_free, 1)
                    step(dve.tensor_tensor(r_a[:, :, :], r_a[:, :, :], onehot[:, :, :], ALU.mult))
                    step(dve.tensor_reduce(pos_f[:, :], r_a[:, :, :], AX_X, ALU.add))
                    step(dve.tensor_copy(pos_i[:, :], pos_f[:, :]))
                    step(dve.tensor_tensor(taken[:, :], taken[:, :], upto[:, :, GT - 1], ALU.add))
                    dve.sem_inc(placed, 1)
                    assert count[0] == F_STEPS, count[0]

            def tables(tiles, first_row, n0, n):
                tile = iota_s[:, 0:n]
                by_tile = over(tile, 2, E)
                is_of, part = has[:, n0:n0 + n, :], t_a[:, 0:n, :]
                link(dve.tensor_tensor_scan(ends[:, :], ones_e[:, :], tiles, 0.0, ALU.mult, ALU.add))
                link(dve.tensor_tensor(starts[:, :], ends[:, :], tiles, ALU.subtract))
                link(dve.tensor_tensor(is_of, over(ends[:, :], 1, n), by_tile, ALU.is_gt))
                link(dve.tensor_tensor(part, over(starts[:, :], 1, n), by_tile, ALU.is_gt))
                link(dve.tensor_tensor(is_of, is_of, part, ALU.subtract))
                link(dve.tensor_tensor(part, is_of, over(iota_s[:, 0:E], 1, n), ALU.mult))
                link(dve.tensor_reduce(tile_f[:, 0:n], part, AX_X, ALU.add))
                link(dve.tensor_copy(eid_i[:, n0:n0 + n], tile_f[:, 0:n]))
                link(dve.scalar_tensor_tensor(out=starts[:, :], in0=starts[:, :], scalar=float(-P), in1=first_row,
                                              op0=ALU.mult, op1=ALU.add))
                link(dve.tensor_tensor(part, is_of, over(starts[:, :], 1, n), ALU.mult))
                link(dve.tensor_reduce(tile_f[:, 0:n], part, AX_X, ALU.add))
                link(dve.tensor_reduce(in_use[:, 0:n], is_of, AX_X, ALU.add))
                link(dve.tensor_scalar(tile_g[:, 0:n], tile, float(P), float(-FILL), ALU.mult, ALU.add))
                link(dve.tensor_tensor(tile_g[:, 0:n], tile_g[:, 0:n], in_use[:, 0:n], ALU.mult))
                link(dve.scalar_tensor_tensor(out=tile_f[:, 0:n], in0=tile_f[:, 0:n], scalar=float(FILL),
                                              in1=tile_g[:, 0:n], op0=ALU.add, op1=ALU.add))
                link(dve.tensor_copy(row_i[:, n0:n0 + n], tile_f[:, 0:n]))

            def early_tables():
                link(dve.tensor_copy(tiles_i[:, :], taken[:, :]))
                link(dve.tensor_scalar(tiles_i[:, :], tiles_i[:, :], P.bit_length() - 1, None, ALU.logical_shift_right))
                link(dve.tensor_copy(tiles_n[:, :], tiles_i[:, :]))
                tables(tiles_n[:, :], region[:, :], 0, EARLY)
                dve.sem_inc(early_ready, 1)

            def late_tables():
                link(dve.tensor_tensor(fill_f[:, :], region[:, :], taken[:, :], ALU.add))
                dve.tensor_copy(fill_i[:, :], fill_f[:, :]).then_inc(fill_ready, 1)
                link(dve.tensor_scalar(tiles_i[:, :], taken[:, :], float(P - 1), None, ALU.add))
                link(dve.tensor_scalar(tiles_i[:, :], tiles_i[:, :], P.bit_length() - 1, None, ALU.logical_shift_right))
                link(dve.tensor_copy(tiles_n[:, :], tiles_i[:, :]))
                link(dve.tensor_reduce(done_early[:, :], has[:, 0:EARLY, :].rearrange("p s e -> p e s"), AX_X, ALU.add))
                link(dve.tensor_tensor(tiles_n[:, :], tiles_n[:, :], done_early[:, :], ALU.subtract))
                link(dve.scalar_tensor_tensor(out=fill_f[:, :], in0=done_early[:, :], scalar=float(P),
                                              in1=region[:, :], op0=ALU.mult, op1=ALU.add))
                tables(tiles_n[:, :], fill_f[:, :], EARLY, NL)
                link(dve.tensor_scalar(used_i[:, :], ends[:, E - 1:E], float(EARLY), None, ALU.add))
                dve.sem_inc(tables_ready, 1)

            def take_logits(g):
                dve.wait_ge(side_ps, task(g, LOGITS) + 1)
                router(g - 1, 6)
                dve.sem_inc(side_free, 1)

            def take_attention(g):
                dve.wait_ge(acc_done, g + 1)
                dve.tensor_copy(att_cur[:, :, :], ps_acc[:, :].rearrange("p (b n) -> p b n", b=GT)
                                ).then_inc(acc_free, 1)
                dve.wait_ge(acc_free, g + 1)

            def beside(g, hp, first, last):
                if hp == 0 and not first:
                    take_attention(g - 1)
                if first and hp < NG - 1:
                    stats_x(hp + 1)
                if first and hp == 2:
                    later_constants()
                if hp == 1 and not last:
                    norm_x(g + 1)
                if hp == 5 and not last:
                    dve.wait_ge(side_free, task(g, TURN_X[1]) + 1)
                    context_low(g + 1, ctx_next)
                    x_low(g + 1)
                if not first:
                    parts = ({0: (0,), 1: (1, 2), 2: (3, 4)} if last
                             else {0: (0,), 2: (1, 2), 3: (3,), 4: (4,)})
                    for part in parts.get(hp, ()):
                        router(g - 1, part)
                kind = kind_of(hp, first, last)
                if kind == NULL_SCORES:
                    dve.wait_ge(side_ps, task(g, kind) + 1)
                    take_null_scores(g + 1, ps_side[:, 0:GT * H])
                    dve.wait_ge(nsn_ready, g + 2)
                    dve.sem_inc(side_free, 1)
                if kind == NULL_OUT:
                    dve.wait_ge(side_ps, task(g, kind) + 1)
                    for b in range(GT):
                        ins = dve.tensor_scalar(nw_rows[:, b, :], ps_side[:, 0:D], rows_of[:, b:b + 1], None, ALU.mult)
                    ins.then_inc(side_free, 1)
                if kind == LOGITS:
                    take_logits(g)
                if kind == COUNTS:
                    router(g - 1, 7)
                if last and hp == 6:
                    early_tables()

            def norm_rows(i, j):
                par, k = j % 2, i * 2 + j // 2
                dve.wait_ge(xs_in[j], 16 * (i + 1))
                dve.wait_ge(xs_turned[par], k)
                dve.tensor_scalar(xn_s[par], xs_sb[j][:, 0:D], xs_sb[j][:, MEAN:MEAN + 1],
                                  xs_sb[j][:, RSTD:RSTD + 1], ALU.subtract, ALU.mult).then_inc(xn_s_ready[par], 1)

            def norm_next(i, j):
                if j + 1 < NB:
                    norm_rows(i, j + 1)
                else:
                    norm_rows(i + 1, 0)

            def take_rows(i, j):
                par, k = j % 2, i * 2 + j // 2
                dve.wait_ge(xs_turned[par], k + 1)
                dve.wait_ge(h_ps[par], 2 * k)
                dve.tensor_copy(xsT[par], ps_x[par].rearrange("p (k n) -> p k n", k=KD)
                                ).then_inc(xsT_ready[par], 1)

            def take_next(i, j):
                if j + 1 < NB:
                    take_rows(i, j + 1)
                else:
                    take_rows(i + 1, 0)

            def take_b1(i, j):
                par, k = j % 2, i * 2 + j // 2
                e = dve.value_load(eid_i[0:1, ds(i * NB + j, 1)], min_val=0, max_val=E - 1)
                dve.wait_ge(h_sb[par], FC * k)
                dve.tensor_copy(b1_cur[par], b1T[:, ds(e * FC, FC)]).then_inc(b1_ready[par], 1)

            def group(g, first=False, last=False):
                for hp in range(HP):
                    n = g * HP + hp
                    pair = slice(2 * hp, 2 * hp + 2)
                    for half in range(2):
                        m, b2 = 2 * n + half, slice(2 * half, 2 * half + 2)
                        null = nsn[:, ds(g * GT + 2 * half, 2), pair]
                        dve.wait_ge(scored, m + 1)
                        dve.tensor_reduce(rowmax[:, b2, :].rearrange("p b h -> p (b h)"),
                                          ps_s[:, half * 512:(half + 1) * 512].rearrange("p (j n) -> p j n", n=P),
                                          AX_X, ALU.max).then_inc(row_max, 1)
                        dve.wait_ge(row_max, m + 1)
                        if not (first and hp == 0):
                            dve.wait_ge(exp_done, m - 1)
                        dve.scalar_tensor_tensor(out=nmax[:, b2, :], in0=rowmax[:, b2, :], scalar=-SCALE, in1=null,
                                                 op0=ALU.mult, op1=ALU.min).then_inc(nmax_ready, 1)
                        dve.wait_ge(nmax_ready, m + 1)
                        dve.tensor_tensor(null_diff[:, b2, :], nmax[:, b2, :], null, ALU.subtract
                                          ).then_inc(diff_ready, 1)
                    for half in range(2):
                        m, b2 = 2 * n + half, slice(2 * half, 2 * half + 2)
                        dve.wait_ge(null_exp_done, m + 1)
                        dve.wait_ge(exp_done, m + 1)
                        dve.tensor_tensor(denom[:, b2, :], sums[:, b2, :], null_exp[:, b2, :], ALU.add
                                          ).then_inc(denom_ready, 1)
                        dve.wait_ge(denom_ready, m + 1)
                        dve.reciprocal(recip[:, b2, :], denom[:, b2, :]).then_inc(recip_ready, 1)
                        dve.wait_ge(recip_ready, m + 1)
                        part = probs[:, half * GT:(half + 1) * GT, :]
                        by = recip[:, b2, :].rearrange("p b h -> p (b h)")
                        dve.tensor_tensor(part, part, over(by, 2, P), ALU.mult).then_inc(probs_ready, 1)
                        if hp == 0 and not first:
                            dve.wait_ge(null_turned, g)
                        dve.tensor_tensor(null_p[:, 0:GT * H].rearrange("p (b h) -> p b h", h=H)[:, b2, pair],
                                          null_exp[:, b2, :], recip[:, b2, :], ALU.mult).then_inc(null_p_ready, 1)
                    if hp + 1 < HP or not last:
                        take_k(n + 1)
                        take_v(n + 1, (hp + 1) % 2, early=(first and hp == 0))
                    dve.wait_ge(probs_turned, 2 * n + 2)
                    if not (first and hp == 0):
                        dve.wait_ge(weighed, n)
                    dve.tensor_copy(probsT[:, GT:2 * GT, :], ps_s[:, 512:1024].rearrange("p (j n) -> p j n", j=GT)
                                    ).then_inc(pT_hi, 1)
                    beside(g, hp, first, last)

            group(0, first=True)
            with dve.Fori(1, NG - 1) as g:
                group(g)
            group(NG - 1, last=True)

            def finish(i, j):
                par, k = j % 2, i * 2 + j // 2
                dve.wait_ge(y_ps[par], k + 1)
                dve.wait_ge(b2_in[j], 16 * (i + 1))
                dve.wait_ge(sent[j], 16 * i)
                dve.tensor_tensor(y_sb[j], ps_y[par], b2_sb[j], ALU.add).then_inc(y_added, 1)
                dve.wait_ge(y_added, i * NB + j + 1)
                dve.wait_ge(xs_in[j], 16 * (i + 1))
                dve.scalar_tensor_tensor(out=y_sb[j], in0=y_sb[j], scalar=xs_sb[j][:, COEF:COEF + 1],
                                         in1=xs_sb[j][:, 0:D], op0=ALU.mult, op1=ALU.add).then_inc(y_ready[par], 1)

            def tile(i, j):
                take_b1(i, j)
                norm_next(i, j)
                take_next(i, j)
                finish(i, j)

            norm_rows(0, 0)
            take_rows(0, 0)
            take_b1(0, 0)
            take_b1(0, 1)
            take_attention(NG - 1)
            router(NG - 1, 0)
            norm_next(0, 0)
            router(NG - 1, 1)
            router(NG - 1, 2)
            take_next(0, 0)
            router(NG - 1, 3)
            finish(0, 0)
            take_b1(0, 2)
            norm_next(0, 1)
            router(NG - 1, 4)
            take_next(0, 1)
            finish(0, 1)
            take_b1(0, 3)
            norm_next(0, 2)
            take_logits(NG)
            take_next(0, 2)
            router(NG - 1, 7)
            finish(0, 2)
            take_b1(1, 0)
            norm_next(0, 3)
            late_tables()
            take_next(0, 3)
            finish(0, 3)
            finish(1, 0)
            norm_next(1, 0)
            take_next(1, 0)
            with dve.Fori(1, NU // NB - 1) as i:
                for ahead, j in ((0, 1), (0, 2), (0, 3), (1, 0)):
                    tile(i + ahead, j)
            for t in range(NU - 3, NU):
                tile(t // NB, t % NB)
            used = tiles_used(dve)
            for t in range(NU, NS):
                with dve.If(used > t):
                    take_b1(t // NB, t % NB)
                    if t + 1 < NS:
                        norm_next(t // NB, t % NB)
                        take_next(t // NB, t % NB)
                    finish(t // NB, t % NB)


_INS = ['x', 'ctx_768', 'mask_BxS2_bf1', 'g_xattn', 'g_ffn', 'L0_xattn_g_norm', 'L0_xattn_null_kv',
        'L0_xattn_Wq', 'L0_xattn_Wkv', 'L0_xattn_Wout', 'L0_xattn_g_out', 'L0_ffn_Wr', 'L0_ffn_W1',
        'L0_ffn_b1', 'L0_ffn_W2', 'L0_ffn_b2']
_OUTS = [((16, 128, 256), 'float32')]


def kernel(**inputs):
    import numpy as _np
    import concourse.bacc as _bacc
    from concourse import mybir as _mybir
    from concourse.bass_utils import run_bass_kernel_spmd as _run

    nc = _bacc.Bacc("TRN2", target_bir_lowering=False, num_devices=1)
    arrays, args = {}, []
    for name in _INS:
        a = _np.ascontiguousarray(inputs[name])
        if a.dtype.kind == "b":
            a = a.view(_np.uint8)
        arrays[f"in_{name}_dram"] = a
        args.append(nc.dram_tensor(f"in_{name}_dram", a.shape, _mybir.dt.from_np(a.dtype), kind="ExternalInput").ap())
    for i, (shape, dtype) in enumerate(_OUTS):
        dt = _mybir.dt.from_np(_np.dtype(dtype))
        args.append(nc.dram_tensor(f"out_{i}_dram", shape, dt, kind="ExternalOutput").ap())
    flamingo_layer(nc, *args)
    r = _run(nc, [arrays], core_ids=[0])
    got = tuple(r.results[0][f"out_{i}_dram"] for i in range(len(_OUTS)))
    return got[0]
```
